# Optimizing a Trainium2 kernel written in Bass

```python
import numpy as np
import jax
import jax.numpy as jnp

def _softmax(x, axis=-1):
    return jax.nn.softmax(x, axis=axis)

def _gelu(x):
    return jax.nn.gelu(x, approximate=True)

def _silu(x):
    return jax.nn.silu(x)

def _sigmoid(x):
    return jax.nn.sigmoid(x)

def _layernorm(x, axis=-1, eps=1e-05):
    m = jnp.mean(x, axis=axis, keepdims=True)
    v = jnp.var(x, axis=axis, keepdims=True)
    return (x - m) / jnp.sqrt(v + eps)

def _scatter_add(tgt, idx, src, axis=0):
    return tgt.at[idx].add(src)

def _segment_sum(src, seg, n):
    return jax.ops.segment_sum(src, seg, n)
kernel_name = 'mk_prb_d1_jaxref_r8_5d4ddb'

def setup_inputs(seed: int=0):
    np.random.seed(seed)
    _w = jnp.asarray

    def _L0_attn_setup():
        import jax, jax.numpy as jnp
        import numpy as np
        B, S, D = (2, 256, 128)
        H, DH = (16, 64)
        SCALE = DH ** (-0.5)
        key = jax.random.key(seed)
        ks = jax.random.split(key, 5)

        def w(k, shape):
            return jax.random.normal(k, shape, dtype=jnp.float32) * 0.02
        return {'x': jax.random.normal(ks[0], (B, S, D), dtype=jnp.float32), 'Wq': w(ks[1], (D, H * DH)), 'Wk': w(ks[2], (D, H * DH)), 'Wv': w(ks[3], (D, H * DH)), 'Wo': w(ks[4], (H * DH, D)), 'bo': jnp.zeros((D,), dtype=jnp.float32)}
    _L0_attn_in = _L0_attn_setup()

    def _L0_ffn_setup():
        import jax, jax.numpy as jnp
        import numpy as np
        B, T, D, E = (4, 128, 128, 8)
        HD = 4 * D
        key = jax.random.key(seed)
        k1, k2, k3, k4 = jax.random.split(key, 4)
        std = 0.5 * D ** (-0.5)
        bound = 3.0 ** 0.5 * std
        x = jax.random.normal(k1, (B, T, D), dtype=jnp.float32)
        router_w = jax.random.normal(k2, (E, D), dtype=jnp.float32) * 0.02
        expert_fc = jax.random.uniform(k3, (E, D, HD), dtype=jnp.float32, minval=-bound, maxval=bound)
        expert_proj = jax.random.normal(k4, (E, D, HD), dtype=jnp.float32) * 0.02
        return {'x': x, 'router_w': router_w, 'expert_fc': expert_fc, 'expert_proj': expert_proj}
    _L0_ffn_in = _L0_ffn_setup()
    _d = {'L0_attn_x': _L0_attn_in['x'], 'L0_attn_Wq': _L0_attn_in['Wq'], 'L0_attn_Wk': _L0_attn_in['Wk'], 'L0_attn_Wv': _L0_attn_in['Wv'], 'L0_attn_Wo': _L0_attn_in['Wo'], 'L0_attn_bo': _L0_attn_in['bo'], 'L0_ffn_router_w': _L0_ffn_in['router_w'], 'L0_ffn_expert_fc': _L0_ffn_in['expert_fc'], 'L0_ffn_expert_proj': _L0_ffn_in['expert_proj']}
    _x0 = _d['L0_attn_x']
    _d['L0_attn_x'] = jax.random.normal(jax.random.fold_in(jax.random.key(seed), 1), (1, 2048, 128), dtype=_x0.dtype)
    del _x0
    return _d

def reference(L0_attn_x, L0_attn_Wq, L0_attn_Wk, L0_attn_Wv, L0_attn_Wo, L0_attn_bo, L0_ffn_router_w, L0_ffn_expert_fc, L0_ffn_expert_proj):

    def _L0_attn_ref(x, Wq, Wk, Wv, Wo, bo):
        import jax, jax.numpy as jnp
        import numpy as np
        B, S, D = (2, 256, 128)
        H, DH = (16, 64)
        SCALE = DH ** (-0.5)
        b, s, _ = x.shape
        q = (x @ Wq).reshape(b, s, H, DH)
        k = (x @ Wk).reshape(b, s, H, DH)
        v = (x @ Wv).reshape(b, s, H, DH)
        scores = jnp.einsum('bqhd,bkhd->bhqk', q, k) * SCALE
        attn = jax.nn.softmax(scores, axis=-1)
        out = jnp.einsum('bhqk,bkhd->bqhd', attn, v).reshape(b, s, H * DH)
        return out @ Wo + bo

    def _L0_ffn_ref(x, router_w, expert_fc, expert_proj):
        import jax, jax.numpy as jnp
        import numpy as np
        B, T, D, E = (4, 128, 128, 8)
        HD = 4 * D
        logits = jnp.einsum('btd,ed->bte', x, router_w)
        probs = jax.nn.softmax(logits, axis=-1)
        expert_ids = jnp.argmax(probs, axis=-1)
        mask = jax.nn.one_hot(expert_ids, E, dtype=x.dtype)
        h = jnp.einsum('btd,edh->ebth', x, expert_fc)
        h = jnp.square(jax.nn.relu(h))
        out_e = jnp.einsum('ebth,edh->ebtd', h, expert_proj)
        output = jnp.einsum('ebtd,bte->btd', out_e, mask)
        return output
    x = L0_attn_x
    xn = _layernorm(x, axis=-1)
    x = x + _L0_attn_ref(xn, L0_attn_Wq, L0_attn_Wk, L0_attn_Wv, L0_attn_Wo, L0_attn_bo) + _L0_ffn_ref(xn, L0_ffn_router_w, L0_ffn_expert_fc, L0_ffn_expert_proj)
    return x

_drawn_inputs = setup_inputs


def setup_inputs(seed=0):
    import zlib

    import numpy as np

    out = dict(_drawn_inputs(seed))
    spreads = {'L0_attn_bo': (0.0, 0.316)}
    factors = {'L0_attn_Wq': 8.0, 'L0_attn_Wk': 8.0, 'L0_attn_Wv': 8.0, 'L0_attn_Wo': 8.0}
    for name, (base, spread) in spreads.items():
        noise = np.random.default_rng([zlib.crc32(name.encode()), seed]).standard_normal(out[name].shape)
        drawn = base * np.exp(spread * noise) if base else spread * noise
        out[name] = jnp.asarray(drawn.astype(out[name].dtype))
    for name, factor in factors.items():
        out[name] = (out[name] * factor).astype(out[name].dtype)
    return out
```

```python
from contextlib import ExitStack

import numpy as np

import concourse.bass as bass
from concourse import mybir

F32 = mybir.dt.float32
F32R = mybir.dt.float32r
ALU = mybir.AluOpType
ACT = mybir.ActivationFunctionType
AX = mybir.AxisListType

S, D, H, DH = 2048, 128, 16, 64
E, HD = 8, 512
P = 128
NT = S // P
QB = 512
JB = S // QB
TB = QB // P
PAIRS = H // 2
NB = PAIRS * JB
NC = HD // P
SCALE = DH ** -0.5
EPS = 1e-5


class Lin:

    def __init__(self, off, coef=0, i=None):
        self.off, self.coef, self.i = off, (coef if i is not None else 0), i

    def __add__(self, k):
        return Lin(self.off + k, self.coef, self.i)

    def __sub__(self, k):
        return self + (-k)

    def __floordiv__(self, k):
        assert self.coef % k == 0
        return Lin(self.off // k, self.coef // k, self.i)

    def __mod__(self, k):
        assert self.coef % k == 0
        return self.off % k

    def place(self, a, r=0):
        v = a * self.off + r
        return v if self.i is None else self.i * (a * self.coef) + v

    def times(self, a, r=0):
        assert self.i is None or a * self.off + r >= 1
        return self.place(a, r)


def wait(eng, sem, value):
    if isinstance(value, int) and value <= 0:
        return
    eng.wait_ge(sem, value)


def address(eng, value):
    return value if isinstance(value, int) else eng.snap(value)


def prepare(nc, t, x, router_wT, bo):
    with ExitStack() as ctx:
        def sb(name, shape, dt=F32):
            return ctx.enter_context(nc.sbuf_tensor(name, shape, dt))

        def sem(name):
            return ctx.enter_context(nc.semaphore(name))

        xs, xc, sq = sb("xs", [P, NT, D]), sb("xc", [P, NT, D]), sb("sq", [P, NT, D])
        bob, rw = sb("bob", [P, D]), sb("rw", [P, E])
        mean, var, std, rstd = (sb(n, [P, NT]) for n in ("mean", "var", "std", "rstd"))
        logit, isel, ramp = sb("logit", [P, NT, E]), sb("isel", [P, NT, E]), sb("ramp", [P, E])
        top = sb("top", [P, NT])
        tp = [ctx.enter_context(nc.psum_tensor(f"tp{b}", [P, QB], F32)) for b in range(2)]
        lg = ctx.enter_context(nc.psum_tensor("lg", [P, NT, E], F32))
        s_x = [sem(f"p_x{j}") for j in range(JB)]
        s_c, s_id, s_v, s_sd, s_xn, s_t, s_f, s_hi, s_lo, s_lg, s_r = (
            sem(f"p_{n}") for n in ("c", "id", "v", "sd", "xn", "t", "f", "hi", "lo", "lg", "r"))

        def tiles(a, j):
            return a[:, j * TB:(j + 1) * TB, :]

        def over(a, n):
            return a.unsqueeze(2).to_broadcast([P, a.shape[1], n])

        with nc.Block() as block:
            @block.sync
            def _(sp):
                xv = x.rearrange("o (t p) d -> p (o t) d", p=P)
                for j in range(JB):
                    sp.dma_start(tiles(xs, j), tiles(xv, j)).then_inc(s_x[j], 16)
                sp.dma_start(rw[:, :], router_wT).then_inc(s_c, 16)
                sp.dma_start(bob[:, :], bo.rearrange("(o d) -> o d", o=1).to_broadcast([P, D])).then_inc(s_c, 16)

            @block.gpsimd
            def _(pool):
                pool.memset(t["ident"][:, :], 0.0).then_inc(s_id, 1)
                pool.wait_ge(s_id, 1)
                pool.affine_select(out=t["ident"][:, :], in_=t["ident"][:, :], compare_op=ALU.not_equal, fill=1.0,
                                   base=0, pattern=[[-1, P]], channel_multiplier=1).then_inc(s_id, 1)
                pool.memset(t["ones"][:, :], 1.0).then_inc(s_id, 1)
                for e in range(E):
                    pool.memset(ramp[:, e:e + 1], float(E - e)).then_inc(s_id, 1)
                pool.wait_ge(s_c, 32)
                for j in range(JB):
                    pool.wait_ge(s_x[j], 16)
                    pool.tensor_tensor(tiles(t["Y"], j), tiles(xs, j), bob[:, :].unsqueeze(1).to_broadcast([P, TB, D]),
                                       ALU.add)

            @block.vector
            def _(dve):
                done = [0]

                def step(ins):
                    done[0] += 1
                    ins.then_inc(s_v, 1)
                    dve.wait_ge(s_v, done[0])

                for j in range(JB):
                    c = slice(j * TB, (j + 1) * TB)
                    dve.wait_ge(s_x[j], 16)
                    step(dve.tensor_reduce(mean[:, c], tiles(xs, j), AX.X, ALU.add))
                    step(dve.tensor_scalar(mean[:, c], mean[:, c], 1.0 / D, None, ALU.mult))
                    step(dve.tensor_tensor(tiles(xc, j), tiles(xs, j), over(mean[:, c], D), ALU.subtract))
                    step(dve.tensor_tensor(tiles(sq, j), tiles(xc, j), tiles(xc, j), ALU.mult))
                    step(dve.tensor_reduce(var[:, c], tiles(sq, j), AX.X, ALU.add))
                    step(dve.tensor_scalar(var[:, c], var[:, c], 1.0 / D, EPS, ALU.mult, ALU.add))
                    dve.wait_ge(s_sd, j + 1)
                    step(dve.reciprocal(rstd[:, c], std[:, c]))
                    dve.tensor_tensor(tiles(xc, j), tiles(xc, j), over(rstd[:, c], D), ALU.mult).then_inc(s_xn, 1)
                for j in range(JB):
                    q = slice(j * QB, (j + 1) * QB)
                    dve.wait_ge(s_hi, j + 1)
                    dve.tensor_tensor(t["xlo"][:, q], t["xT"][:, q], t["xhi"][:, q], ALU.subtract).then_inc(s_lo, 1)
                dve.wait_ge(s_lg, NT)
                dve.wait_ge(s_id, 3 + E)
                step(dve.tensor_copy(logit[:, :, :], lg[:, :, :]))
                step(dve.tensor_reduce(top[:, :], logit[:, :, :], AX.X, ALU.max))
                step(dve.tensor_tensor(isel[:, :, :], logit[:, :, :], over(top[:, :], E), ALU.is_equal))
                step(dve.tensor_tensor(isel[:, :, :], isel[:, :, :], ramp[:, :].unsqueeze(1).to_broadcast([P, NT, E]), ALU.mult))
                step(dve.tensor_reduce(top[:, :], isel[:, :, :], AX.X, ALU.max))
                step(dve.tensor_tensor(t["mask"][:, :, :].rearrange("p e t -> p t e"), isel[:, :, :], over(top[:, :], E), ALU.is_equal))

            @block.tensor
            def _(pe):
                pe.wait_ge(s_id, 2)
                for j in range(JB):
                    pe.wait_ge(s_xn, j + 1)
                    if j >= 2:
                        pe.wait_ge(s_hi, j - 1)
                    for k in range(TB):
                        mm = pe.transpose(tp[j % 2][:, k * P:(k + 1) * P], xc[:, j * TB + k, :], t["ident"][:, :])
                    mm.then_inc(s_t, 1)
                pe.wait_ge(s_c, 32)
                pe.wait_ge(s_f, JB)
                for k in range(NT):
                    pe.matmul(lg[:, k, :], t["xT"][:, k * P:(k + 1) * P], rw[:, :], start=True, stop=True).then_inc(s_lg, 1)

            @block.scalar
            def _(act):
                for j in range(JB):
                    act.wait_ge(s_v, 7 * j + 6)
                    act.activation(std[:, j * TB:(j + 1) * TB], var[:, j * TB:(j + 1) * TB], ACT.Sqrt).then_inc(s_sd, 1)
                for j in range(JB):
                    q = slice(j * QB, (j + 1) * QB)
                    act.wait_ge(s_t, j + 1)
                    act.activation(t["xT"][:, q], tp[j % 2][:, :], ACT.Copy).then_inc(s_f, 1)
                    act.wait_ge(s_f, j + 1)
                    act.activation(t["xhi"][:, q], tp[j % 2][:, :], ACT.Copy).then_inc(s_hi, 1)


def experts(nc, t, fc, projT):
    B = 32
    with ExitStack() as ctx:
        def sb(name, shape, dt=F32):
            return ctx.enter_context(nc.sbuf_tensor(name, shape, dt))

        def sem(name):
            return ctx.enter_context(nc.semaphore(name))

        w1 = [sb(f"w1_{k}", [P, HD]) for k in range(2)]
        w1hi = [sb(f"w1hi{k}", [P, HD], F32R) for k in range(2)]
        w1lo = [sb(f"w1lo{k}", [P, HD], F32R) for k in range(2)]
        w2 = [sb(f"w2_{k}", [P, NC, D]) for k in range(2)]
        mk = [sb(f"mk{k}", [P, NT]) for k in range(2)]
        rl = [sb(f"rl{k}", [P, QB]) for k in range(2)]
        h2 = [sb(f"h2_{k}", [P, QB]) for k in range(2 * NC)]
        hp = [ctx.enter_context(nc.psum_tensor(f"hp{k}", [P, QB], F32)) for k in range(2)]
        yp = [ctx.enter_context(nc.psum_tensor(f"yp{k}", [P, QB], F32)) for k in range(2)]
        s_w = [sem(f"f_w{k}") for k in range(2)]
        s_wh, s_wl, s_mk, s_fc, s_rl, s_h2, s_pj, s_y = (
            sem(f"f_{n}") for n in ("wh", "wl", "mk", "fc", "rl", "h2", "pj", "y"))

        def loop(eng, body):
            with eng.Fori(0, E // 2) as i:
                for k in range(2):
                    body(Lin(k, 2, i))

        with nc.Block() as block:
            @block.sync
            def _(sp):
                def body(e):
                    k = e % 2
                    ev = address(sp, e.place(1))
                    wait(sp, s_pj, e.times(JB, B - JB))
                    sp.dma_start(w1[k][:, :], fc[bass.ds(ev, 1), :, :].rearrange("e d h -> d (e h)")).then_inc(s_w[k], 16)
                    sp.dma_start(w2[k][:, :, :], projT[bass.ds(ev, 1), :, :].rearrange("e (c p) d -> p (e c) d", p=P)).then_inc(s_w[k], 16)
                loop(sp, body)

            @block.scalar
            def _(act):
                act.sem_inc(s_rl, B)
                act.sem_inc(s_wh, B)

                def body(e):
                    k = e % 2
                    wait(act, s_w[k], (e // 2).times(32, 32))
                    wait(act, s_fc, e.times(JB * NC, B - JB * NC))
                    act.activation(w1hi[k][:, :], w1[k][:, :], ACT.Copy).then_inc(s_wh, 1)
                    for g in range(JB * NC):
                        wait(act, s_fc, e.times(JB * NC, B + g + 1))
                        wait(act, s_h2, e.times(JB * NC, B + g - 1))
                        act.activation(rl[g % 2][:, :], hp[g % 2][:, :], ACT.Relu).then_inc(s_rl, 1)
                loop(act, body)

            @block.vector
            def _(dve):
                dve.sem_inc(s_h2, B)
                dve.sem_inc(s_wl, B)
                dve.sem_inc(s_y, B)

                def split(e):
                    k = e % 2
                    wait(dve, s_wh, e.times(1, B + 1))
                    dve.tensor_tensor(w1lo[k][:, :], w1[k][:, :], w1hi[k][:, :], ALU.subtract).then_inc(s_wl, 1)
                    dve.tensor_copy(mk[k][:, :], t["mask"][:, bass.ds(e.place(1), 1), :].rearrange("p e t -> p (e t)")).then_inc(s_mk, 1)

                def add(e, j):
                    k = e % 2
                    wait(dve, s_pj, e.times(JB, B + j + 1))
                    wait(dve, s_mk, e.times(1, 1))
                    for q in range(TB):
                        tile = j * TB + q
                        ins = dve.scalar_tensor_tensor(out=t["Y"][:, tile, :], in0=yp[j % 2][:, q * P:(q + 1) * P],
                                                       scalar=mk[k][:, tile:tile + 1], in1=t["Y"][:, tile, :],
                                                       op0=ALU.mult, op1=ALU.add)
                    ins.then_inc(s_y, 1)

                def body(e):
                    split(e)
                    for j in range(JB):
                        for c in range(NC):
                            g = j * NC + c
                            wait(dve, s_rl, e.times(JB * NC, B + g + 1))
                            wait(dve, s_pj, e.times(JB, B + j - 1))
                            dve.tensor_tensor(h2[g % (2 * NC)][:, :], rl[g % 2][:, :], rl[g % 2][:, :], ALU.mult).then_inc(s_h2, 1)
                        if j:
                            add(e, j - 1)
                    add(e, JB - 1)
                loop(dve, body)

            @block.tensor
            def _(pe):
                pe.sem_inc(s_fc, B)
                pe.sem_inc(s_pj, B)

                def project(e, j):
                    wait(pe, s_h2, e.times(JB * NC, B + (j + 1) * NC))
                    wait(pe, s_y, e.times(JB, B + j - 1))
                    for q in range(TB):
                        for c in range(NC):
                            mm = pe.matmul(yp[j % 2][:, q * P:(q + 1) * P], h2[(j * NC + c) % (2 * NC)][:, q * P:(q + 1) * P],
                                           w2[e % 2][:, c, :], start=(c == 0), stop=(c == NC - 1))
                    mm.then_inc(s_pj, 1)

                def body(e):
                    k = e % 2
                    wait(pe, s_wl, e.times(1, B + 1))
                    for j in range(JB):
                        q = slice(j * QB, (j + 1) * QB)
                        for c in range(NC):
                            g = j * NC + c
                            wait(pe, s_rl, e.times(JB * NC, B + g - 1))
                            w = slice(c * P, (c + 1) * P)
                            pe.matmul(hp[g % 2][:, :], w1hi[k][:, w], t["xhi"][:, q], start=True, stop=False)
                            pe.matmul(hp[g % 2][:, :], w1lo[k][:, w], t["xhi"][:, q], start=False, stop=False)
                            pe.matmul(hp[g % 2][:, :], w1hi[k][:, w], t["xlo"][:, q], start=False, stop=True).then_inc(s_fc, 1)
                        if j:
                            project(e, j - 1)
                    project(e, JB - 1)
                loop(pe, body)


LEAD = 4
UNITS = 16
RING = 4
AT_DEN, AT_KV, AT_Q, AT_WO, AT_NM, AT_T = 2, (4, 6), 8, 10, 12, 13
LOOP = 8
TURNS = (NB - 1) // LOOP


def attention(nc, t, wq, wk, wv, wo, out):
    with ExitStack() as ctx:
        def sb(name, shape, dt=F32):
            return ctx.enter_context(nc.sbuf_tensor(name, shape, dt))

        def sem(name):
            return ctx.enter_context(nc.semaphore(name))

        def bank(name, n=1):
            return ctx.enter_context(nc.psum_tensor(name, [P, n * QB], F32))

        own = [slice(0, DH), slice(DH, P)]
        other = [slice(DH, P), slice(0, DH)]
        maxrow = [slice(DH, DH + 1), slice(0, 1)]
        K1, K2 = ([[sb(f"{n}_{k}{h}", [P, S], F32R) for h in range(2)] for k in range(2)] for n in ("K1", "K2"))
        Q1, Q2 = ([[sb(f"{n}_{k}{h}", [P, QB], F32R) for h in range(2)] for k in range(JB)] for n in ("Q1", "Q2"))
        V = [sb(f"V{k}", [P, NT, P]) for k in range(2)]
        qhi, qlo, khi, klo = (sb(n, [P, QB], F32R) for n in ("qhi", "qlo", "khi", "klo"))
        wraw = [sb(f"wraw{k}", [P, 3, P]) for k in range(2)]
        whi = [sb(f"whi{k}", [P, 2, P], F32R) for k in range(2)]
        wlo = [sb(f"wlo{k}", [P, 2, P], F32R) for k in range(2)]
        wo_s = [sb(f"wo{k}", [P, D]) for k in range(2)]
        EX = [[sb(f"ex{h}{k}", [P, QB]) for k in range(RING)] for h in range(2)]
        acc = [[sb(f"acc{h}{k}", [P, QB]) for k in range(2)] for h in range(2)]
        osb, rd, on = sb("osb", [P, QB]), sb("rd", [P, QB]), sb("on", [P, QB])
        mx, nm = sb("mx", [P, 2, UNITS]), sb("nm", [P, 2, UNITS // 2])
        mrow = sb("mrow", [UNITS // 2, P], F32R)
        MB = [bank(f"MB{k}", 2) for k in range(2)]
        SB = [bank(f"SB{h}") for h in range(2)]
        OB, XB = bank("OB"), bank("XB")

        t_s, t_m, t_pv, t_q, t_k, t_v, t_den, t_wo, t_nm = (
            sem(f"t_{n}") for n in ("s", "m", "pv", "q", "k", "v", "den", "wo", "nm"))
        a_e, a_o, a_q, a_k, a_w, a_v, a_nm = (sem(f"a_{n}") for n in ("e", "o", "q", "k", "w", "v", "nm"))
        v_m, v_nm, v_q, v_k, v_w, v_a, v_rd, v_y = (
            sem(f"v_{n}") for n in ("m", "nm", "q", "k", "w", "a", "rd", "y"))
        g_a, g_on, g_c = sem("g_a"), sem("g_on"), sem("g_c")
        d_q, d_nm = ([sem(f"d_{n}{k}") for k in range(JB)] for n in ("q", "nm"))
        d_k, d_w, d_wo = ([sem(f"d_{n}{k}") for k in range(2)] for n in ("k", "w", "wo"))
        d_out = sem("d_out")
        QD, KD = 6 * 16, 6 * 16

        def unit(n, kt):
            g = UNITS + kt + LEAD
            return n + g // UNITS, g % UNITS

        def added(n, kt):
            return n.times(NT - 1, max(kt, 1))

        def kv_jobs(n):
            j = n % JB
            return [("k" if j < 2 else "v", n // JB + 1, 2 * (j % 2) + c) for c in range(2)]

        def schedule(eng, first, block, last):
            first()
            block(Lin(0))
            with eng.Fori(0, TURNS) as i:
                for b in range(1, LOOP + 1):
                    block(Lin(b, LOOP, i))
            for n in range(1 + LOOP * TURNS, NB):
                block(Lin(n))
            last()

        def before(n, limit):
            return n.i is not None or n.off < limit

        def q_ready(eng, m):
            wait(eng, d_q[m % JB], (m // JB).times(QD, QD))

        def k_ready(eng, pair):
            wait(eng, d_k[pair % 2], (pair // 2).times(JB * KD, JB * KD))

        with nc.Block() as block:
            @block.sync
            def _(sp):
                def load_w(pair):
                    k, cols = pair % 2, bass.ds(address(sp, pair.place(P)), P)
                    wait(sp, t_v, pair.times(JB, -JB))
                    for n, w in enumerate((wq, wk, wv)):
                        sp.dma_start(wraw[k][:, n, :], w[:, cols]).then_inc(d_w[k], 16)

                def load_wo(pair):
                    rows = bass.ds(address(sp, pair.place(P)), P)
                    if pair.i is not None or pair.off:
                        wait(sp, t_wo, pair.times(JB, 1 - JB))
                    sp.dma_start(wo_s[pair % 2][:, :], wo[rows, :]).then_inc(d_wo[pair % 2], 16)

                def copy(dst, src, s):
                    sp.dma_start(dst.bitcast(F32), src.bitcast(F32)).then_inc(s, 16)

                def spread_q(m):
                    k = m % JB
                    wait(sp, v_q, m.times(1, 1))
                    for h in range(2):
                        copy(Q1[k][h][own[h], :], qhi[own[h], :], d_q[k])
                        copy(Q2[k][h][own[h], :], qhi[own[h], :], d_q[k])
                        copy(Q1[k][h][other[h], :], qlo[own[h], :], d_q[k])

                def spread_k(pair, c):
                    k, q = pair % 2, slice(c * QB, (c + 1) * QB)
                    wait(sp, v_k, pair.times(JB, c + 1))
                    for h in range(2):
                        copy(K1[k][h][own[h], q], khi[own[h], :], d_k[k])
                        copy(K1[k][h][other[h], q], khi[own[h], :], d_k[k])
                        copy(K2[k][h][own[h], q], klo[own[h], :], d_k[k])

                def place_max(m):
                    k = m % JB
                    wait(sp, a_nm, m.times(1, 1))
                    wait(sp, g_c, 1)
                    for h in range(2):
                        copy(Q2[k][h][maxrow[h], :], mrow[h * TB:(h + 1) * TB, :], d_nm[k])

                def first():
                    for pair in range(2):
                        load_w(Lin(pair))
                    load_wo(Lin(0))
                    for c in range(JB):
                        spread_k(Lin(0), c)
                    for m in range(3):
                        spread_q(Lin(m))
                    place_max(Lin(0))

                def one(n):
                    pair = n // JB
                    if before(n, NB - JB):
                        for kind, p, c in kv_jobs(n):
                            if kind == "k":
                                spread_k(p, c)
                    if n % JB == 1:
                        if before(n, NB - 2 * JB):
                            load_w(pair + 2)
                    if before(n, NB - 3):
                        spread_q(n + 3)
                    if n % JB == 1 and before(n, NB - JB):
                        load_wo(pair + 1)
                    if before(n, NB - 1):
                        place_max(n + 1)

                def last():
                    ov = out.rearrange("o (t p) d -> p (o t) d", p=P)
                    for j in range(JB):
                        sp.wait_ge(v_y, NB - JB + j + 1)
                        sp.dma_start(ov[:, j * TB:(j + 1) * TB, :], t["Y"][:, j * TB:(j + 1) * TB, :]).then_inc(d_out, 16)
                    sp.wait_ge(d_out, 16 * JB)

                schedule(sp, first, one, last)

            @block.gpsimd
            def _(pool):
                def add(n, kt):
                    a = acc[1][n % 2]
                    wait(pool, a_e, n.times(2 * NT, 2 * kt + 2))
                    if kt == 1:
                        src = EX[1][0]
                    else:
                        wait(pool, g_a, n.times(NT - 1, kt - 1))
                        src = a
                    pool.tensor_tensor(a[:, :], src[:, :], EX[1][kt % RING][:, :], ALU.add).then_inc(g_a, 1)

                def normalise(n):
                    wait(pool, v_rd, n.times(1, 1))
                    wait(pool, a_o, n.times(1, 1))
                    pool.tensor_tensor(on[:, :], osb[:, :], rd[:, :], ALU.mult).then_inc(g_on, 1)

                def first():
                    ins = []
                    for h in range(2):
                        for k in range(2):
                            pool.memset(K2[k][h][other[h], :].bitcast(F32), 0.0)
                        for k in range(JB):
                            ins.append(pool.memset(Q2[k][h][other[h], :].bitcast(F32), 0.0))
                    ins[-1].then_inc(g_c, 1)
                    pool.wait_ge(g_c, 1)
                    for h in range(2):
                        for k in range(2):
                            ins = pool.memset(K2[k][h][maxrow[h], :].bitcast(F32), 1.0)
                    ins.then_inc(g_c, 1)

                def one(n):
                    for kt in range(1, NT):
                        add(n, kt)
                        if kt == 5 and not (n.i is None and n.off == 0):
                            normalise(n - 1)

                schedule(pool, first, one, lambda: normalise(Lin(NB - 1)))

            @block.scalar
            def _(act):
                def exps(n, kt):
                    for h in range(2):
                        wait(act, t_s, n.times(2 * NT, 2 * kt + h + 1))
                        old = (n, kt - RING) if kt >= RING else (n - 1, kt - RING + NT)
                        if n.i is not None or n.off > 0 or kt >= RING:
                            wait(act, t_pv, old[0].times(NT, old[1] + 1))
                            wait(act, (v_a, g_a)[h], added(*old))
                        act.activation(EX[h][kt % RING][:, :], SB[h][:, :], ACT.Exp).then_inc(a_e, 1)

                def split_w(pair):
                    k = pair % 2
                    wait(act, d_w[k], (pair // 2).times(48, 48))
                    wait(act, t_q, pair.times(JB, -JB))
                    act.activation(whi[k][:, :, :], wraw[k][:, 0:2, :], ACT.Copy).then_inc(a_w, 1)

                def high_q(m):
                    wait(act, t_q, m.times(1, 1))
                    if before(m, 1) and m.i is None:
                        pass
                    else:
                        q_ready(act, m - 1)
                    act.activation(qhi[:, :], XB[:, :], ACT.Copy, scale=SCALE).then_inc(a_q, 1)

                def kv(kind, pair, c):
                    if kind == "k":
                        wait(act, t_k, pair.times(JB, c + 1))
                        if c:
                            wait(act, d_k[pair % 2], (pair // 2).times(JB * KD, c * KD))
                        elif not (pair.i is None and pair.off == 0):
                            k_ready(act, pair - 1)
                        act.activation(khi[:, :], XB[:, :], ACT.Copy).then_inc(a_k, 1)
                    else:
                        wait(act, t_v, pair.times(JB, c + 1))
                        wait(act, t_pv, pair.times(NT * JB, 1 - NT * JB))
                        act.activation(V[pair % 2][:, c * TB:(c + 1) * TB, :].rearrange("p t d -> p (t d)"), XB[:, :],
                                       ACT.Copy).then_inc(a_v, 1)

                def max_rows(m):
                    wait(act, t_nm, m.times(1, 1))
                    if not (m.i is None and m.off == 0):
                        old = m - 1
                        wait(act, d_nm[old % JB], (old // JB).times(32, 32))
                    act.activation(mrow[:, :], XB[0:UNITS // 2, 0:P], ACT.Copy).then_inc(a_nm, 1)

                def take_o(n):
                    wait(act, t_pv, n.times(NT, NT))
                    act.activation(osb[:, :], OB[:, :], ACT.Copy).then_inc(a_o, 1)

                def first():
                    split_w(Lin(0))
                    for c in range(JB):
                        kv("k", Lin(0), c)
                        kv("v", Lin(0), c)
                    for m in range(3):
                        high_q(Lin(m))
                    max_rows(Lin(0))

                def one(n):
                    for kt in range(NT):
                        exps(n, kt)
                        if kt == 0 and not (n.i is None and n.off == 0):
                            take_o(n - 1)
                        if kt == 1 and n % JB == 0 and before(n, NB - JB):
                            split_w(n // JB + 1)
                        if kt in AT_KV and before(n, NB - JB):
                            kv(*kv_jobs(n)[AT_KV.index(kt)])
                        if kt == AT_Q and before(n, NB - 3):
                            high_q(n + 3)
                        if kt == AT_T and before(n, NB - 1):
                            max_rows(n + 1)

                schedule(act, first, one, lambda: take_o(Lin(NB - 1)))

            @block.vector
            def _(dve):
                def maxima(m, u):
                    wait(dve, t_m, m.times(UNITS, u + 1))
                    dve.tensor_reduce(mx[:, m % 2, u:u + 1], MB[u % 2][:, :], AX.X, ALU.max).then_inc(v_m, 1)

                def minus_max(m):
                    wait(dve, v_m, m.times(UNITS, UNITS))
                    wait(dve, t_nm, m.times(1, -1))
                    dve.tensor_reduce(nm[:, m % 2, :], mx[:, m % 2, :].rearrange("p (a b) -> p a b", b=2), AX.X,
                                      ALU.max, negate=True).then_inc(v_nm, 1)

                def add(n, kt):
                    a = acc[0][n % 2]
                    wait(dve, a_e, n.times(2 * NT, 2 * kt + 1))
                    if kt == 1:
                        src = EX[0][0]
                    else:
                        wait(dve, v_a, n.times(NT - 1, kt - 1))
                        src = a
                    dve.tensor_tensor(a[:, :], src[:, :], EX[0][kt % RING][:, :], ALU.add).then_inc(v_a, 1)

                def low_w(pair):
                    k = pair % 2
                    wait(dve, a_w, pair.times(1, 1))
                    dve.tensor_tensor(wlo[k][:, :, :], wraw[k][:, 0:2, :], whi[k][:, :, :], ALU.subtract).then_inc(v_w, 1)

                def low_q(m):
                    wait(dve, a_q, m.times(1, 1))
                    dve.scalar_tensor_tensor(out=qlo[:, :], in0=XB[:, :], scalar=SCALE, in1=qhi[:, :],
                                             op0=ALU.mult, op1=ALU.subtract).then_inc(v_q, 1)

                def low_k(pair, c):
                    wait(dve, a_k, pair.times(JB, c + 1))
                    dve.tensor_tensor(klo[:, :], XB[:, :], khi[:, :], ALU.subtract).then_inc(v_k, 1)

                def invert(n):
                    wait(dve, t_den, n.times(1, 1))
                    dve.reciprocal(rd[:, :], XB[:, :]).then_inc(v_rd, 1)

                def sum_up(n):
                    wait(dve, t_wo, n.times(1, 1))
                    y = t["Y"][:, (n % JB) * TB:(n % JB + 1) * TB, :].rearrange("p t d -> p (t d)")
                    dve.tensor_tensor(y, XB[:, :], y, ALU.add).then_inc(v_y, 1)

                def first():
                    low_w(Lin(0))
                    for c in range(JB):
                        low_k(Lin(0), c)
                    for m in range(3):
                        low_q(Lin(m))
                    for u in range(UNITS):
                        maxima(Lin(0), u)
                    minus_max(Lin(0))
                    for u in range(LEAD):
                        maxima(Lin(1), u)

                def one(n):
                    start = n.i is None and n.off == 0
                    for kt in range(NT):
                        m, u = unit(n, kt)
                        if before(m, NB):
                            maxima(m, u)
                        if kt > 1:
                            add(n, kt - 1)
                        if kt == 0 and not start:
                            add(n - 1, NT - 1)
                        if kt == 1 and n % JB == 0 and before(n, NB - JB):
                            low_w(n // JB + 1)
                        if kt == AT_DEN and not start:
                            invert(n - 1)
                        if kt in AT_KV and before(n, NB - JB):
                            kind, pair, c = kv_jobs(n)[AT_KV.index(kt)]
                            if kind == "k":
                                low_k(pair, c)
                        if kt == AT_Q and before(n, NB - 3):
                            low_q(n + 3)
                        if kt == AT_WO and not start:
                            sum_up(n - 1)
                        if kt == AT_NM and before(n, NB - 1):
                            minus_max(n + 1)

                def last():
                    add(Lin(NB - 1), NT - 1)
                    invert(Lin(NB - 1))
                    sum_up(Lin(NB - 1))

                schedule(dve, first, one, last)

            @block.tensor
            def _(pe):
                freed = [None]

                def take_spare(sem_, value):
                    if freed[0]:
                        wait(pe, *freed[0])
                    freed[0] = (sem_, value)

                def scores(n, kt):
                    par, k, keys = (n // JB) % 2, n % JB, slice(kt * P, (kt + 1) * P)
                    for h in range(2):
                        wait(pe, a_e, n.times(2 * NT, 2 * kt + h - 1))
                        if kt == 0:
                            q_ready(pe, n)
                        pe.matmul(SB[h][:, :], K1[par][h][:, keys], Q1[k][h][:, :], start=True, stop=False)
                        if kt == 0 and h == 0:
                            wait(pe, d_nm[k], (n // JB).times(32, 32))
                            wait(pe, g_c, 2)
                        pe.matmul(SB[h][:, :], K2[par][h][:, keys], Q2[k][h][:, :], start=False, stop=True).then_inc(t_s, 1)

                def max_unit(m, u):
                    h, q, half = u // 8, u % 8 // 2, u % 2
                    par, k = (m // JB) % 2, m % JB
                    wait(pe, v_m, m.times(UNITS, u - 1))
                    if u == 0:
                        q_ready(pe, m)
                        k_ready(pe, m // JB)
                    for c in range(2):
                        keys = slice((2 * half + c) * QB, (2 * half + c + 1) * QB)
                        mm = pe.matmul(MB[u % 2][:, c * QB:(c + 1) * QB], Q1[k][h][:, q * P:(q + 1) * P],
                                       K1[par][h][:, keys], start=True, stop=True)
                    mm.then_inc(t_m, 1)

                def times_v(n, kt):
                    wait(pe, a_e, n.times(2 * NT, 2 * kt + 2))
                    if kt == 0:
                        wait(pe, a_o, n.times(1))
                        wait(pe, a_v, (n // JB).times(JB, JB))
                    for h in range(2):
                        mm = pe.matmul(OB[own[h], :], V[(n // JB) % 2][:, kt, own[h]], EX[h][kt % RING][:, :],
                                       start=(kt == 0), stop=(kt == NT - 1))
                    mm.then_inc(t_pv, 1)

                def split_product(w, par, c):
                    q = slice(c * QB, (c + 1) * QB)
                    pe.matmul(XB[:, :], whi[par][:, w, :], t["xhi"][:, q], start=True, stop=False)
                    pe.matmul(XB[:, :], wlo[par][:, w, :], t["xhi"][:, q], start=False, stop=False)
                    return pe.matmul(XB[:, :], whi[par][:, w, :], t["xlo"][:, q], start=False, stop=True)

                def make_q(m):
                    take_spare(v_q, m.times(1, 1))
                    wait(pe, v_w, (m // JB).times(1, 1))
                    split_product(0, (m // JB) % 2, m % JB).then_inc(t_q, 1)

                def make_kv(kind, pair, c):
                    if kind == "k":
                        take_spare(v_k, pair.times(JB, c + 1))
                        wait(pe, v_w, pair.times(1, 1))
                        split_product(1, pair % 2, c).then_inc(t_k, 1)
                    else:
                        take_spare(a_v, pair.times(JB, c + 1))
                        wait(pe, d_w[pair % 2], (pair // 2).times(48, 48))
                        for k in range(TB):
                            tok = slice((c * TB + k) * P, (c * TB + k + 1) * P)
                            mm = pe.matmul(XB[:, k * P:(k + 1) * P], t["xT"][:, tok], wraw[pair % 2][:, 2, :],
                                           start=True, stop=True)
                        mm.then_inc(t_v, 1)

                def denominators(n):
                    take_spare(v_rd, n.times(1, 1))
                    wait(pe, v_a, n.times(NT - 1, NT - 1))
                    wait(pe, g_a, n.times(NT - 1, NT - 1))
                    for h in range(2):
                        mm = pe.matmul(XB[own[h], :], t["ones"][:, :], acc[h][n % 2][:, :], start=True, stop=True)
                    mm.then_inc(t_den, 1)

                def project(n):
                    take_spare(v_y, n.times(1, 1))
                    pair = n // JB
                    wait(pe, g_on, n.times(1, 1))
                    wait(pe, d_wo[pair % 2], (pair // 2).times(16, 16))
                    for q in range(TB):
                        mm = pe.matmul(XB[:, q * P:(q + 1) * P], on[:, q * P:(q + 1) * P], wo_s[pair % 2][:, :],
                                       start=True, stop=True)
                    mm.then_inc(t_wo, 1)

                def turn_max(m):
                    take_spare(a_nm, m.times(1, 1))
                    wait(pe, v_nm, m.times(1, 1))
                    pe.transpose(XB[0:UNITS // 2, 0:P], nm[:, m % 2, :], t["ident"][:, :]).then_inc(t_nm, 1)

                def first():
                    for c in range(JB):
                        make_kv("k", Lin(0), c)
                        make_kv("v", Lin(0), c)
                    for m in range(3):
                        make_q(Lin(m))
                    for u in range(UNITS):
                        max_unit(Lin(0), u)
                    turn_max(Lin(0))
                    for u in range(LEAD):
                        max_unit(Lin(1), u)

                def one(n):
                    start = n.i is None and n.off == 0
                    if n.i is not None and n.off == 1:
                        freed[0] = (a_nm, n.times(1, 1))
                    for kt in range(NT):
                        scores(n, kt)
                        m, u = unit(n, kt)
                        if before(m, NB):
                            max_unit(m, u)
                        if kt == AT_DEN and not start:
                            denominators(n - 1)
                        if kt in AT_KV and before(n, NB - JB):
                            make_kv(*kv_jobs(n)[AT_KV.index(kt)])
                        if kt == AT_Q and before(n, NB - 3):
                            make_q(n + 3)
                        if kt == AT_WO and not start:
                            project(n - 1)
                        if kt == AT_T and before(n, NB - 1):
                            turn_max(n + 1)
                        if kt:
                            times_v(n, kt - 1)
                        elif not start:
                            times_v(n - 1, NT - 1)
                    if n.i is not None and n.off == LOOP:
                        freed[0] = (a_nm, LOOP * TURNS + 2)

                def last():
                    times_v(Lin(NB - 1), NT - 1)
                    denominators(Lin(NB - 1))
                    project(Lin(NB - 1))

                schedule(pe, first, one, last)


def build(nc, x, wq, wk, wv, wo, bo, router_wT, fc, projT, out):
    with ExitStack() as ctx:
        def sb(name, shape, dt=F32):
            return ctx.enter_context(nc.sbuf_tensor(name, shape, dt))

        t = {
            "Y": sb("Y", [P, NT, D]),
            "xT": sb("xT", [P, S]),
            "xhi": sb("xhi", [P, S], F32R),
            "xlo": sb("xlo", [P, S], F32R),
            "mask": sb("mask", [P, E, NT]),
            "ident": sb("ident", [P, P]),
            "ones": sb("ones", [P, DH]),
        }
        prepare(nc, t, x, router_wT, bo)
        experts(nc, t, fc, projT)
        attention(nc, t, wq, wk, wv, wo, out)


def kernel(L0_attn_x, L0_attn_Wq, L0_attn_Wk, L0_attn_Wv, L0_attn_Wo, L0_attn_bo, L0_ffn_router_w, L0_ffn_expert_fc,
           L0_ffn_expert_proj):
    import concourse.bacc as bacc
    from concourse.bass_utils import run_bass_kernel_spmd

    nc = bacc.Bacc("TRN2", target_bir_lowering=False, num_devices=1)
    ins = {
        "x": L0_attn_x, "wq": L0_attn_Wq, "wk": L0_attn_Wk, "wv": L0_attn_Wv, "wo": L0_attn_Wo, "bo": L0_attn_bo,
        "router_wT": np.asarray(L0_ffn_router_w).T, "fc": L0_ffn_expert_fc,
        "projT": np.asarray(L0_ffn_expert_proj).transpose(0, 2, 1),
    }
    ins = {n: np.ascontiguousarray(a) for n, a in ins.items()}
    aps = [nc.dram_tensor(n, a.shape, mybir.dt.from_np(a.dtype), kind="ExternalInput").ap() for n, a in ins.items()]
    out = nc.dram_tensor("out", (1, S, D), F32, kind="ExternalOutput").ap()
    build(nc, *aps, out)
    r = run_bass_kernel_spmd(nc, [ins], core_ids=[0])
    return r.results[0]["out"]
```

```python
from contextlib import ExitStack

import numpy as np

import concourse.bass as bass
from concourse import mybir

F32 = mybir.dt.float32
F32R = mybir.dt.float32r
U32 = mybir.dt.uint32
I32 = mybir.dt.int32
ALU = mybir.AluOpType
ACT = mybir.ActivationFunctionType
AX = mybir.AxisListType

S, D, H, DH = 2048, 128, 16, 64
E, HD = 8, 512
P = 128
NT = S // P
QB = 512
JB = S // QB
TB = QB // P
PAIRS = H // 2
NB = PAIRS * JB
NC = HD // P
SCALE = DH ** -0.5
EPS = 1e-5


class Lin:

    def __init__(self, off, coef=0, i=None):
        self.off, self.coef, self.i = off, (coef if i is not None else 0), i

    def __add__(self, k):
        return Lin(self.off + k, self.coef, self.i)

    def __sub__(self, k):
        return self + (-k)

    def __floordiv__(self, k):
        assert self.coef % k == 0
        return Lin(self.off // k, self.coef // k, self.i)

    def __mod__(self, k):
        assert self.coef % k == 0
        return self.off % k

    def place(self, a, r=0):
        v = a * self.off + r
        return v if self.i is None else self.i * (a * self.coef) + v

    def times(self, a, r=0):
        assert self.i is None or a * self.off + r >= 1
        return self.place(a, r)


def wait(eng, sem, value):
    if isinstance(value, int) and value <= 0:
        return
    eng.wait_ge(sem, value)


def address(eng, value):
    return value if isinstance(value, int) else eng.snap(value)


LEAD = 4
UNITS = 16
RING = 4
AT_DEN, AT_KV, AT_Q, AT_WO, AT_NM, AT_T = 2, (4, 10), 6, 8, 12, 13
AT_TOK, AT_UP, AT_DOWN = 5, 7, 11
LOOP = 8
TURNS = (NB - 1) // LOOP
TILES = LOOP * TURNS
assert TILES >= NT + E - 1
AT_LOGIT, AT_RANK = 2, 5
BACK = (4, 5, 6, 7)


def layer(nc, x, wq, wk, wv, wo, bo, router_wT, fc, projT, out):
    with ExitStack() as ctx:
        def sb(name, shape, dt=F32):
            return ctx.enter_context(nc.sbuf_tensor(name, shape, dt))

        def sem(name):
            return ctx.enter_context(nc.semaphore(name))

        def bank(name, n=1):
            return ctx.enter_context(nc.psum_tensor(name, [P, n * QB], F32))

        Y = sb("Y", [P, NT, D])
        xT, xhi, xlo = sb("xT", [P, S]), sb("xhi", [P, S], F32R), sb("xlo", [P, S], F32R)
        ident, ones = sb("ident", [P, P]), sb("ones", [P, P])

        own = [slice(0, DH), slice(DH, P)]
        other = [slice(DH, P), slice(0, DH)]
        maxrow = [slice(DH, DH + 1), slice(0, 1)]
        K1, K2 = ([[sb(f"{n}_{k}{h}", [P, S], F32R) for h in range(2)] for k in range(2)] for n in ("K1", "K2"))
        Q1, Q2 = ([[sb(f"{n}_{k}{h}", [P, QB], F32R) for h in range(2)] for k in range(JB)] for n in ("Q1", "Q2"))
        V = [sb(f"V{k}", [P, NT, P]) for k in range(2)]
        qhi, qlo, khi, klo = (sb(n, [P, QB], F32R) for n in ("qhi", "qlo", "khi", "klo"))
        wraw = [sb(f"wraw{k}", [P, 3, P]) for k in range(2)]
        whi = [sb(f"whi{k}", [P, 2, P], F32R) for k in range(2)]
        wlo = [sb(f"wlo{k}", [P, 2, P], F32R) for k in range(2)]
        wo_s = [sb(f"wo{k}", [P, D]) for k in range(2)]
        EX = [[sb(f"ex{h}{k}", [P, QB]) for k in range(RING)] for h in range(2)]
        acc = [[sb(f"acc{h}{k}", [P, QB]) for k in range(2)] for h in range(2)]
        xn = V[1]
        total_x, minus_mean, var, std, rstd, shift = (
            sb(n_, [P, NT]) for n_ in ("total_x", "minus_mean", "var", "std", "rstd", "shift"))
        bob, eps = sb("bob", [P, D]), sb("eps", [P, 1])
        rw = sb("rw", [P, E])
        pick, mask, total, cum, place = (sb(n_, [P, E, NT]) for n_ in ("pick", "mask", "total", "cum", "place"))
        top, slot = sb("top", [P, NT]), sb("slot", [P, NT], U32)
        tiles_of, end, start_ = (sb(n_, [P, E]) for n_ in ("tiles_of", "end", "start"))
        past, owner, owner_i = sb("past", [P, TILES, E]), sb("owner", [P, TILES]), sb("owner_i", [P, TILES], I32)
        before_p, gate = sb("before_p", [P, P]), sb("gate", [P, E, NT])
        falling, tokens_in, tile_no, one_e = (
            sb(n_, [P, k]) for n_, k in (("falling", E), ("tokens_in", NT), ("tile_no", TILES), ("one_e", E)))
        tok, tokT, w1, w2 = sb("tok", [P, D]), sb("tokT", [P, P]), sb("w1", [P, HD]), sb("w2", [P, NC, D])
        up, hid, res = sb("up", [P, NC * P]), sb("hid", [P, NC * P]), sb("res", [P, D])
        sorted_x = nc.dram_tensor("sorted_x", (TILES * P, D), F32, kind="Internal").ap()
        sorted_y = nc.dram_tensor("sorted_y", (TILES * P, D), F32, kind="Internal").ap()
        osb, rd, on = sb("osb", [P, QB]), sb("rd", [P, QB]), sb("on", [P, QB])
        mx, nm = sb("mx", [P, 2, UNITS]), sb("nm", [P, 2, UNITS // 2])
        mrow = sb("mrow", [UNITS // 2, P], F32R)
        MB = [bank(f"MB{k}", 2) for k in range(2)]
        SB = [bank(f"SB{h}") for h in range(2)]
        OB, XB = bank("OB"), bank("XB")

        t_s, t_m, t_pv, t_q, t_k, t_v, t_den, t_wo, t_nm = (
            sem(f"t_{n}") for n in ("s", "m", "pv", "q", "k", "v", "den", "wo", "nm"))
        a_e, a_o, a_q, a_k, a_w, a_v, a_nm = (sem(f"a_{n}") for n in ("e", "o", "q", "k", "w", "v", "nm"))
        v_m, v_nm, v_q, v_k, v_w, v_a, v_rd, v_y = (
            sem(f"v_{n}") for n in ("m", "nm", "q", "k", "w", "a", "rd", "y"))
        g_a, g_on, g_c = sem("g_a"), sem("g_on"), sem("g_c")
        d_x, d_c = [sem(f"d_x{j}") for j in range(JB)], sem("d_c")
        v_ln, v_mean, v_rs, v_sh, a_xn, a_sq, a_std, t_x, a_x, v_lo, g_y, g_i = (sem(n_) for n_ in (
            "v_ln", "v_mean", "v_rs", "v_sh", "a_xn", "a_sq", "a_std", "t_x", "a_x", "v_lo", "g_y", "g_i"))
        a_q0 = sem("a_q0")
        d_zero, t_lg, t_rk, v_r, v_mask, v_slot, v_own, d_sort = (
            sem(n_) for n_ in ("d_zero", "t_lg", "t_rk", "v_r", "v_mask", "v_slot", "v_own", "d_sort"))
        d_tile, t_tok, t_up, t_down, a_tok, a_up, a_res, g_hid, d_res, d_back, v_back = (
            sem(n_) for n_ in ("d_tile", "t_tok", "t_up", "t_down", "a_tok", "a_up", "a_res", "g_hid", "d_res", "d_back", "v_back"))
        d_q, d_nm = ([sem(f"d_{n}{k}") for k in range(JB)] for n in ("q", "nm"))
        d_k, d_w, d_wo = ([sem(f"d_{n}{k}") for k in range(2)] for n in ("k", "w", "wo"))
        d_k0 = [sem(f"d_k0{c}") for c in range(JB)]
        d_out = sem("d_out")
        QD, KD = 6 * 16, 6 * 16

        def unit(n, kt):
            g = UNITS + kt + LEAD
            return n + g // UNITS, g % UNITS

        def added(n, kt):
            return n.times(NT - 1, max(kt, 1))

        def kv_jobs(n):
            j = n % JB
            return [("k" if j < 2 else "v", n // JB + 1, 2 * (j % 2) + c) for c in range(2)]

        def schedule(eng, first, block, last):
            first()
            block(Lin(0))
            with eng.Fori(0, TURNS) as i:
                for b in range(1, LOOP + 1):
                    block(Lin(b, LOOP, i))
            for n in range(1 + LOOP * TURNS, NB):
                block(Lin(n))
            last()

        def before(n, limit):
            return n.i is not None or n.off < limit

        def q_ready(eng, m):
            wait(eng, d_q[m % JB], (m // JB).times(QD, QD))

        BETWEEN = {1: ("v", 0), 3: ("v", 1), 5: ("v", 2), 7: ("v", 3), 9: ("q", 1), 12: ("q", 2)}
        START = [SB[0], SB[1], OB, XB]
        TX = [MB[j % 2][:, j // 2 * QB:(j // 2 + 1) * QB] for j in range(JB)]
        ORDER = list(range(0, UNITS, 2)) + list(range(1, UNITS, 2))

        def k_ready(eng, pair):
            wait(eng, d_k[pair % 2], (pair // 2).times(JB * KD, JB * KD))

        def chunk(a, j):
            return a[:, j * TB:(j + 1) * TB, :]

        def over(a, n):
            return a.unsqueeze(2).to_broadcast([P, a.shape[1], n])

        def under(a, n):
            return a.unsqueeze(1).to_broadcast([P, n, a.shape[1]])

        def has_tile(n):
            return n.i is not None or 0 < n.off <= TILES

        with nc.Block() as block:
            @block.sync
            def _(sp):
                def load_w(pair):
                    k, cols = pair % 2, bass.ds(address(sp, pair.place(P)), P)
                    wait(sp, t_v, pair.times(JB, -JB))
                    for n, w in enumerate((wq, wk, wv)):
                        sp.dma_start(wraw[k][:, n, :], w[:, cols]).then_inc(d_w[k], 16)

                def load_wo(pair):
                    rows = bass.ds(address(sp, pair.place(P)), P)
                    if pair.i is not None or pair.off:
                        wait(sp, t_wo, pair.times(JB, 1 - JB))
                    sp.dma_start(wo_s[pair % 2][:, :], wo[rows, :]).then_inc(d_wo[pair % 2], 16)

                def copy(dst, src, s):
                    sp.dma_start(dst.bitcast(F32), src.bitcast(F32)).then_inc(s, 16)

                def spread_q(m):
                    k = m % JB
                    wait(sp, v_q, m.times(1, 1))
                    for h in range(2):
                        copy(Q1[k][h][own[h], :], qhi[own[h], :], d_q[k])
                        copy(Q2[k][h][own[h], :], qhi[own[h], :], d_q[k])
                        copy(Q1[k][h][other[h], :], qlo[own[h], :], d_q[k])

                def spread_k(pair, c):
                    k, q = pair % 2, slice(c * QB, (c + 1) * QB)
                    wait(sp, v_k, pair.times(JB, c + 1))
                    for h in range(2):
                        copy(K1[k][h][own[h], q], khi[own[h], :], d_k[k])
                        copy(K1[k][h][other[h], q], khi[own[h], :], d_k[k])
                        copy(K2[k][h][own[h], q], klo[own[h], :], d_k[k])

                def spread_k0(c):
                    q = slice(c * QB, (c + 1) * QB)
                    sp.wait_ge(a_k, c + 1)
                    for h in range(2):
                        copy(K1[0][h][other[h], q], K1[0][h][own[h], q], d_k0[c])

                def spread_q0():
                    sp.wait_ge(v_q, 1)
                    for h in range(2):
                        copy(Q1[0][h][other[h], :], qlo[own[h], :], d_q[0])
                    sp.wait_ge(a_q0, 1)
                    sp.sem_inc(d_q[0], QD - 32)

                def place_max(m):
                    k = m % JB
                    wait(sp, a_nm, m.times(1, 1))
                    wait(sp, g_c, 1)
                    for h in range(2):
                        copy(Q2[k][h][maxrow[h], :], mrow[h * TB:(h + 1) * TB, :], d_nm[k])

                def load_tile(r):
                    e = sp.value_load(owner_i[0:1, bass.ds(r.place(1), 1)], min_val=0, max_val=E - 1)
                    sp.dma_start(tok[:, :], sorted_x[bass.ds(r.place(P), P), :]).then_inc(d_tile, 16)
                    sp.dma_start(w1[:, :], fc[bass.ds(e, 1), :, :].rearrange("e d h -> d (e h)")).then_inc(d_tile, 16)
                    sp.dma_start(w2[:, :, :], projT[bass.ds(e, 1), :, :].rearrange("e (c p) d -> p (e c) d", p=P))\
                      .then_inc(d_tile, 16)

                def store_tile(r):
                    wait(sp, a_res, r.times(1, 1))
                    sp.dma_start(sorted_y[bass.ds(r.place(P), P), :], res[:, :]).then_inc(d_res, 16)

                def first():
                    xv = x.rearrange("o (t p) d -> p (o t) d", p=P)
                    for j in range(JB):
                        sp.dma_start(chunk(Y, j), chunk(xv, j)).then_inc(d_x[j], 16)
                    load_w(Lin(0))
                    sp.dma_start(rw[:, :], router_wT).then_inc(d_c, 16)
                    sp.dma_start(bob[:, :], bo.rearrange("(o d) -> o d", o=1).to_broadcast([P, D])).then_inc(d_c, 16)
                    for c in range(JB):
                        spread_k0(c)
                        if c == 0:
                            spread_q0()
                    load_w(Lin(1))
                    load_wo(Lin(0))
                    sp.wait_ge(g_i, 1)
                    sp.dma_start(sorted_x.rearrange("(r p) d -> p r d", p=P), under(res[:, :], TILES)).then_inc(d_res, 16)
                    for c in range(JB):
                        sp.wait_ge(d_k0[c], 32)
                    sp.wait_ge(v_k, JB)
                    sp.sem_inc(d_k[0], JB * KD)
                    for m in (1, 2):
                        spread_q(Lin(m))
                    place_max(Lin(0))

                def one(n):
                    pair = n // JB
                    if has_tile(n):
                        sp.wait_ge(d_sort, 16 * NT)
                        sp.wait_ge(v_own, 1)
                        load_tile(n - 1)
                    if n % JB == 1:
                        if before(n, NB - 2 * JB):
                            load_w(pair + 2)
                        if before(n, NB - JB):
                            load_wo(pair + 1)
                    spread = kv_jobs(n) if before(n, NB - JB) and n % JB < 2 else [None, None]
                    if spread[0]:
                        spread_k(*spread[0][1:])
                    if before(n, NB - 3):
                        spread_q(n + 3)
                    if spread[1]:
                        spread_k(*spread[1][1:])
                    if has_tile(n):
                        store_tile(n - 1)
                    if before(n, NB - 1):
                        place_max(n + 1)

                def last():
                    ov = out.rearrange("o (t p) d -> p (o t) d", p=P)
                    for j in range(JB):
                        sp.wait_ge(v_y, NB - JB + j + 1)
                        sp.dma_start(ov[:, j * TB:(j + 1) * TB, :], Y[:, j * TB:(j + 1) * TB, :]).then_inc(d_out, 16)
                    sp.wait_ge(d_out, 16 * JB)

                schedule(sp, first, one, last)

            @block.gpsimd
            def _(pool):
                def add(n, kt):
                    a = acc[1][n % 2]
                    wait(pool, a_e, n.times(2 * NT, 2 * kt + 2))
                    if kt == 1:
                        src = EX[1][0]
                    else:
                        wait(pool, g_a, n.times(NT - 1, kt - 1))
                        src = a
                    pool.tensor_tensor(a[:, :], src[:, :], EX[1][kt % RING][:, :], ALU.add).then_inc(g_a, 1)

                def normalise(n):
                    wait(pool, v_rd, n.times(1, 1))
                    wait(pool, a_o, n.times(1, 1))
                    pool.tensor_tensor(on[:, :], osb[:, :], rd[:, :], ALU.mult).then_inc(g_on, 1)

                def square(r):
                    wait(pool, a_up, r.times(1, 1))
                    pool.tensor_tensor(hid[:, :], up[:, :], up[:, :], ALU.mult).then_inc(g_hid, 1)

                def indexed(k):
                    return bass.IndirectOffsetOnAxis(ap=slot[:, k:k + 1], axis=0)

                def sort_tokens(ks):
                    pool.wait_ge(v_slot, 1)
                    pool.wait_ge(d_res, 16)
                    for k in ks:
                        pool.indirect_dma_start(sorted_x, indexed(k), xn[:, k, :], None).then_inc(d_sort, 16)

                def fetch_results(ks):
                    pool.wait_ge(d_res, 16 * (TILES + 1))
                    pool.wait_ge(t_pv, NT * (NB - JB))
                    for k in ks:
                        pool.indirect_dma_start(V[0][:, k, :], None, sorted_y, indexed(k)).then_inc(d_back, 16)

                def first():
                    pool.memset(res[:, :], 0.0).then_inc(g_i, 1)
                    pool.memset(eps[:, :], EPS).then_inc(g_i, 1)
                    pool.memset(ident[:, :], 0.0).then_inc(g_i, 1)
                    pool.wait_ge(g_i, 3)
                    pool.affine_select(out=ident[:, :], in_=ident[:, :], compare_op=ALU.not_equal, fill=1.0,
                                       base=0, pattern=[[-1, P]], channel_multiplier=1).then_inc(g_i, 1)
                    pool.memset(ones[:, :], 1.0).then_inc(g_i, 1)
                    pool.wait_ge(g_i, 5)
                    pool.affine_select(out=before_p[:, :], in_=ones[:, :], compare_op=ALU.is_gt, fill=0.0,
                                       base=0, pattern=[[1, P]], channel_multiplier=-1)
                    pool.memset(one_e[:, :], 1.0)
                    pool.memset(gate[:, :, 1:NT], 1.0)
                    pool.memset(gate[:, :, 0:1], 0.0)
                    for a, n, step, base in ((falling, E, -1, E), (tokens_in, NT, P, 0), (tile_no, TILES, 1, 0)):
                        ins = pool.iota(a[:, :], [[step, n]], base=base, channel_multiplier=0,
                                        allow_small_or_imprecise_dtypes=True)
                    ins.then_inc(g_i, 1)
                    pool.wait_ge(g_i, 6)
                    ins = []
                    for h in range(2):
                        for k in range(2):
                            pool.memset(K2[k][h][other[h], :].bitcast(F32), 0.0)
                        for k in range(JB):
                            ins.append(pool.memset(Q2[k][h][other[h], :].bitcast(F32), 0.0))
                    ins[-1].then_inc(g_c, 1)
                    pool.wait_ge(g_c, 1)
                    for h in range(2):
                        for k in range(2):
                            ins = pool.memset(K2[k][h][maxrow[h], :].bitcast(F32), 1.0)
                    ins.then_inc(g_c, 1)
                    pool.wait_ge(g_c, 2)
                    pool.wait_ge(d_c, 32)
                    for j in range(JB):
                        pool.wait_ge(a_xn, j + 1)
                        pool.tensor_tensor(chunk(Y, j), chunk(Y, j), under(bob[:, :], TB), ALU.add).then_inc(g_y, 1)

                def one(n):
                    for kt in range(1, NT):
                        add(n, kt)
                        if kt == 5 and not (n.i is None and n.off == 0):
                            normalise(n - 1)
                        if kt == AT_UP + 1 and has_tile(n):
                            square(n - 1)
                        if kt >= 8 and n.i is None and n.off == 0:
                            sort_tokens((2 * kt - NT, 2 * kt - NT + 1))
                        if n.i is None and n.off == NB - JB:
                            fetch_results((kt,) if kt > 1 else (0, 1))

                schedule(pool, first, one, lambda: normalise(Lin(NB - 1)))

            @block.scalar
            def _(act):
                def exps(n, kt):
                    for h in range(2):
                        wait(act, t_s, n.times(2 * NT, 2 * kt + h + 1))
                        old = (n, kt - RING) if kt >= RING else (n - 1, kt - RING + NT)
                        if n.i is not None or n.off > 0 or kt >= RING:
                            wait(act, t_pv, old[0].times(NT, old[1] + 1))
                            wait(act, (v_a, g_a)[h], added(*old))
                        act.activation(EX[h][kt % RING][:, :], SB[h][:, :], ACT.Exp).then_inc(a_e, 1)

                def split_w(pair):
                    k = pair % 2
                    wait(act, d_w[k], (pair // 2).times(48, 48))
                    wait(act, t_q, pair.times(JB, -JB))
                    act.activation(whi[k][:, :, :], wraw[k][:, 0:2, :], ACT.Copy).then_inc(a_w, 1)

                def high_q(m, XB=XB):
                    wait(act, t_q, m.times(1, 1))
                    if before(m, 1) and m.i is None:
                        pass
                    else:
                        q_ready(act, m - 1)
                    act.activation(qhi[:, :], XB[:, :], ACT.Copy, scale=SCALE).then_inc(a_q, 1)

                def kv(kind, pair, c, XB=XB):
                    if kind == "k":
                        wait(act, t_k, pair.times(JB, c + 1))
                        if c:
                            wait(act, d_k[pair % 2], (pair // 2).times(JB * KD, c * KD))
                        elif not (pair.i is None and pair.off == 0):
                            k_ready(act, pair - 1)
                        act.activation(khi[:, :], XB[:, :], ACT.Copy).then_inc(a_k, 1)
                    else:
                        wait(act, t_v, pair.times(JB, c + 1))
                        wait(act, t_pv, pair.times(NT * JB, 1 - NT * JB))
                        act.activation(V[pair % 2][:, c * TB:(c + 1) * TB, :].rearrange("p t d -> p (t d)"), XB[:, :],
                                       ACT.Copy).then_inc(a_v, 1)

                def max_rows(m):
                    wait(act, t_nm, m.times(1, 1))
                    if not (m.i is None and m.off == 0):
                        old = m - 1
                        wait(act, d_nm[old % JB], (old // JB).times(32, 32))
                    act.activation(mrow[:, :], XB[0:UNITS // 2, 0:P], ACT.Copy).then_inc(a_nm, 1)

                def take_o(n):
                    wait(act, t_pv, n.times(NT, NT))
                    act.activation(osb[:, :], OB[:, :], ACT.Copy).then_inc(a_o, 1)

                def root(j):
                    act.wait_ge(v_mean, j + 1)
                    for k in range(j * TB, (j + 1) * TB):
                        ins = act.activation(EX[1][j][:, k % TB * D:(k % TB + 1) * D], Y[:, k, :], ACT.Square,
                                             bias=minus_mean[:, k:k + 1], accum_out=var[:, k:k + 1])
                    ins.then_inc(a_sq, 1)
                    act.wait_ge(a_sq, j + 1)
                    c = slice(j * TB, (j + 1) * TB)
                    act.activation(std[:, c], var[:, c], ACT.Sqrt, bias=eps[:, 0:1], scale=1.0 / D).then_inc(a_std, 1)

                def rows(j):
                    act.wait_ge(v_sh, j + 1)
                    for k in range(j * TB, (j + 1) * TB):
                        ins = act.activation(xn[:, k, :], Y[:, k, :], ACT.Identity, bias=shift[:, k:k + 1],
                                             scale=rstd[:, k:k + 1])
                    ins.then_inc(a_xn, 1)

                def turned(j):
                    q = slice(j * QB, (j + 1) * QB)
                    act.wait_ge(t_x, j + 1)
                    act.activation(xhi[:, q], TX[j], ACT.Copy)
                    act.activation(xT[:, q], TX[j], ACT.Copy).then_inc(a_x, 1)

                def high_k0(c):
                    act.wait_ge(t_k, c + 1)
                    for h in range(2):
                        ins = act.activation(K1[0][h][own[h], c * QB:(c + 1) * QB], START[c][own[h], :], ACT.Copy)
                    ins.then_inc(a_k, 1)

                def high_q0():
                    act.wait_ge(t_q, 1)
                    for h in range(2):
                        ins = act.activation(Q1[0][h][own[h], :], SB[0][own[h], :], ACT.Copy, scale=SCALE)
                    ins.then_inc(a_q, 1)
                    act.wait_ge(a_q, 1)
                    for h in range(2):
                        ins = act.activation(Q2[0][h][own[h], :], Q1[0][h][own[h], :], ACT.Copy)
                    ins.then_inc(a_q0, 1)

                def copy_tokens(r):
                    wait(act, t_tok, r.times(1, 1))
                    act.activation(tokT[:, :], XB[:, 0:P], ACT.Copy).then_inc(a_tok, 1)

                def rectify(r):
                    wait(act, t_up, r.times(1, 1))
                    act.activation(up[:, :], XB[:, :], ACT.Relu).then_inc(a_up, 1)

                def take_result(r):
                    wait(act, t_down, r.times(1, 1))
                    wait(act, d_res, r.times(16, 16))
                    act.activation(res[:, :], XB[:, 0:D], ACT.Copy).then_inc(a_res, 1)

                def first():
                    act.wait_ge(g_i, 2)
                    act.activation(std[:, 0:1], eps[:, 0:1], ACT.Sqrt)
                    for s_ in range(JB + 3):
                        if s_ < JB:
                            root(s_)
                        if s_ == 1:
                            split_w(Lin(0))
                        if 1 <= s_ < JB + 1:
                            rows(s_ - 1)
                        if 2 <= s_ < JB + 2:
                            turned(s_ - 2)
                        if s_ >= 3:
                            high_k0(s_ - 3)
                            if s_ == 3:
                                high_q0()
                    for u in range(UNITS):
                        if u in BETWEEN:
                            kind, c = BETWEEN[u]
                            if kind == "v":
                                kv("v", Lin(0), c)
                            else:
                                high_q(Lin(c))
                    max_rows(Lin(0))

                def one(n):
                    for kt in range(NT):
                        exps(n, kt)
                        if has_tile(n):
                            if kt == AT_TOK:
                                copy_tokens(n - 1)
                            if kt == AT_UP:
                                rectify(n - 1)
                            if kt == AT_DOWN:
                                take_result(n - 1)
                        if kt == 0 and not (n.i is None and n.off == 0):
                            take_o(n - 1)
                        if kt == 1 and n % JB == 0 and before(n, NB - JB):
                            split_w(n // JB + 1)
                        if kt in AT_KV and before(n, NB - JB):
                            kv(*kv_jobs(n)[AT_KV.index(kt)])
                        if kt == AT_Q and before(n, NB - 3):
                            high_q(n + 3)
                        if kt == AT_T and before(n, NB - 1):
                            max_rows(n + 1)

                schedule(act, first, one, lambda: take_o(Lin(NB - 1)))

            @block.vector
            def _(dve):
                def maxima(m, i, u=None):
                    u = i if u is None else u
                    wait(dve, t_m, m.times(UNITS, i + 1))
                    dve.tensor_reduce(mx[:, m % 2, u:u + 1], MB[i % 2][:, :], AX.X, ALU.max).then_inc(v_m, 1)

                def minus_max(m):
                    wait(dve, v_m, m.times(UNITS, UNITS))
                    wait(dve, t_nm, m.times(1, -1))
                    dve.tensor_reduce(nm[:, m % 2, :], mx[:, m % 2, :].rearrange("p (a b) -> p a b", b=2), AX.X,
                                      ALU.max, negate=True).then_inc(v_nm, 1)

                def add(n, kt):
                    a = acc[0][n % 2]
                    wait(dve, a_e, n.times(2 * NT, 2 * kt + 1))
                    if kt == 1:
                        src = EX[0][0]
                    else:
                        wait(dve, v_a, n.times(NT - 1, kt - 1))
                        src = a
                    dve.tensor_tensor(a[:, :], src[:, :], EX[0][kt % RING][:, :], ALU.add).then_inc(v_a, 1)

                def low_w(pair):
                    k = pair % 2
                    wait(dve, a_w, pair.times(1, 1))
                    dve.tensor_tensor(wlo[k][:, :, :], wraw[k][:, 0:2, :], whi[k][:, :, :], ALU.subtract).then_inc(v_w, 1)

                def means(j):
                    c = slice(j * TB, (j + 1) * TB)
                    dve.wait_ge(d_x[j], 16)
                    dve.tensor_reduce(total_x[:, c], chunk(Y, j), AX.X, ALU.add).then_inc(v_ln, 1)
                    dve.wait_ge(v_ln, j + 1)
                    dve.tensor_scalar(minus_mean[:, c], total_x[:, c], -1.0 / D, None, ALU.mult).then_inc(v_mean, 1)

                def scales(j):
                    c = slice(j * TB, (j + 1) * TB)
                    dve.wait_ge(a_std, j + 1)
                    dve.reciprocal(rstd[:, c], std[:, c]).then_inc(v_rs, 1)
                    dve.wait_ge(v_rs, j + 1)
                    dve.tensor_tensor(shift[:, c], minus_mean[:, c], rstd[:, c], ALU.mult).then_inc(v_sh, 1)

                def low_x(j):
                    q = slice(j * QB, (j + 1) * QB)
                    dve.wait_ge(a_x, j + 1)
                    dve.tensor_tensor(xlo[:, q], xT[:, q], xhi[:, q], ALU.subtract).then_inc(v_lo, 1)

                def low_k0(c):
                    q = slice(c * QB, (c + 1) * QB)
                    dve.wait_ge(a_k, c + 1)
                    for h in range(2):
                        ins = dve.tensor_tensor(K2[0][h][own[h], q], START[c][own[h], :], K1[0][h][own[h], q], ALU.subtract)
                    ins.then_inc(v_k, 1)

                def low_q0():
                    dve.wait_ge(a_q, 1)
                    for h in range(2):
                        ins = dve.scalar_tensor_tensor(out=qlo[own[h], :], in0=SB[0][own[h], :], scalar=SCALE,
                                                       in1=Q1[0][h][own[h], :], op0=ALU.mult, op1=ALU.subtract)
                    ins.then_inc(v_q, 1)

                routed = [0]

                def step(ins):
                    routed[0] += 1
                    ins.then_inc(v_r, 1)
                    dve.wait_ge(v_r, routed[0])

                def choose():
                    logit = XB[:, 0:NT * E].rearrange("p (t e) -> p e t", e=E)
                    by_tile = logit.rearrange("p e t -> p t e")
                    dve.wait_ge(t_lg, 1)
                    dve.wait_ge(g_i, 6)
                    step(dve.tensor_reduce(top[:, :], by_tile, AX.X, ALU.max))
                    step(dve.tensor_tensor(pick[:, :, :], logit, under(top[:, :], E), ALU.is_equal))
                    step(dve.tensor_tensor(pick[:, :, :], pick[:, :, :], over(falling[:, :], NT), ALU.mult))
                    step(dve.tensor_reduce(top[:, :], pick[:, :, :].rearrange("p e t -> p t e"), AX.X, ALU.max))
                    dve.tensor_tensor(mask[:, :, :], pick[:, :, :], under(top[:, :], E), ALU.is_equal).then_inc(v_mask, 1)

                def rank():
                    earlier = XB[:, 0:NT * E].rearrange("p (e t) -> p e t", e=E)
                    dve.wait_ge(t_rk, 1)
                    step(dve.tensor_copy(total[:, :, :].rearrange("p e t -> p (e t)"), XB[:, NT * E:2 * NT * E]))
                    dve.tensor_copy(place[:, :, :], earlier).then_inc(v_mask, 1)
                    step(dve.tensor_tensor_scan(cum[:, :, :].rearrange("p e t -> p (e t)"), gate[:, :, :].rearrange("p e t -> p (e t)"),
                                                total[:, :, :].rearrange("p e t -> p (e t)"), 0.0, ALU.mult, ALU.add))
                    dve.wait_ge(v_mask, 2)
                    step(dve.tensor_tensor(place[:, :, :], place[:, :, :], cum[:, :, :], ALU.add))
                    step(dve.tensor_tensor(place[:, :, :], place[:, :, :], total[:, :, :], ALU.subtract))
                    step(dve.tensor_tensor(total[:, :, :], cum[:, :, NT - 1:NT].to_broadcast([P, E, NT]),
                                           under(tokens_in[:, :], E), ALU.is_gt))
                    step(dve.tensor_reduce(tiles_of[:, :], total[:, :, :], AX.X, ALU.add))
                    step(dve.tensor_tensor_scan(end[:, :], one_e[:, :], tiles_of[:, :], 0.0, ALU.mult, ALU.add))
                    step(dve.tensor_tensor(start_[:, :], end[:, :], tiles_of[:, :], ALU.subtract))
                    step(dve.scalar_tensor_tensor(out=place[:, :, :], in0=over(start_[:, :], NT), scalar=float(P),
                                                  in1=place[:, :, :], op0=ALU.mult, op1=ALU.add))
                    step(dve.tensor_tensor(place[:, :, :], place[:, :, :], mask[:, :, :], ALU.mult))
                    step(dve.tensor_reduce(top[:, :], place[:, :, :].rearrange("p e t -> p t e"), AX.X, ALU.add))
                    dve.tensor_copy(slot[:, :], top[:, :]).then_inc(v_slot, 1)
                    step(dve.tensor_tensor(past[:, :, :], over(tile_no[:, :], E), under(end[:, :], TILES), ALU.is_ge))
                    step(dve.tensor_reduce(owner[:, :], past[:, :, :], AX.X, ALU.add))
                    dve.tensor_scalar(owner_i[:, :], owner[:, :], float(E - 1), None, ALU.min).then_inc(v_own, 1)

                def take_back(j):
                    dve.wait_ge(d_back, 16 * NT)
                    dve.wait_ge(v_y, NB - JB)
                    dve.tensor_tensor(chunk(Y, j), chunk(Y, j), chunk(V[0], j), ALU.add).then_inc(v_back, 1)

                def low_q(m, XB=XB):
                    wait(dve, a_q, m.times(1, 1))
                    dve.scalar_tensor_tensor(out=qlo[:, :], in0=XB[:, :], scalar=SCALE, in1=qhi[:, :],
                                             op0=ALU.mult, op1=ALU.subtract).then_inc(v_q, 1)

                def low_k(pair, c, XB=XB):
                    wait(dve, a_k, pair.times(JB, c + 1))
                    dve.tensor_tensor(klo[:, :], XB[:, :], khi[:, :], ALU.subtract).then_inc(v_k, 1)

                def invert(n):
                    wait(dve, t_den, n.times(1, 1))
                    dve.reciprocal(rd[:, :], XB[:, :]).then_inc(v_rd, 1)

                def sum_up(n):
                    wait(dve, t_wo, n.times(1, 1))
                    if n.i is None and n.off == NB - JB:
                        dve.wait_ge(v_back, JB)
                    y = Y[:, (n % JB) * TB:(n % JB + 1) * TB, :].rearrange("p t d -> p (t d)")
                    dve.tensor_tensor(y, XB[:, :], y, ALU.add).then_inc(v_y, 1)

                def first():
                    means(0)
                    means(1)
                    for s_ in range(1, JB + 3):
                        if s_ < JB + 1:
                            scales(s_ - 1)
                        if s_ < JB - 1:
                            means(s_ + 1)
                        if s_ == 1:
                            low_w(Lin(0))
                        if 2 <= s_ < JB + 2:
                            low_x(s_ - 2)
                        if s_ >= 3:
                            low_k0(s_ - 3)
                        if s_ == 3:
                            low_q0()
                    for u in range(UNITS):
                        maxima(Lin(0), u, ORDER[u])
                        if u in BETWEEN and BETWEEN[u][0] == "q":
                            low_q(Lin(BETWEEN[u][1]))
                    minus_max(Lin(0))
                    for u in range(LEAD - 1):
                        maxima(Lin(1), u)

                def one(n):
                    start = n.i is None and n.off == 0
                    for kt in range(NT):
                        m, u = unit(n, kt - 1)
                        if before(m, NB):
                            maxima(m, u)
                        if kt > 1:
                            add(n, kt - 1)
                        if kt == 0 and not start:
                            add(n - 1, NT - 1)
                        if kt == 1 and n % JB == 0 and before(n, NB - JB):
                            low_w(n // JB + 1)
                        if kt == AT_DEN and not start:
                            invert(n - 1)
                        if kt in AT_KV and before(n, NB - JB):
                            kind, pair, c = kv_jobs(n)[AT_KV.index(kt)]
                            if kind == "k":
                                low_k(pair, c)
                        if start and kt == AT_LOGIT:
                            choose()
                        if start and kt == AT_RANK:
                            rank()
                        if n.i is None and n.off == NB - JB + 1 and kt in BACK:
                            take_back(BACK.index(kt))
                        if kt == AT_Q and before(n, NB - 3):
                            low_q(n + 3)
                        if kt == AT_WO:
                            if start:
                                dve.wait_ge(g_y, JB)
                            else:
                                sum_up(n - 1)
                        if kt == AT_NM and before(n, NB - 1):
                            minus_max(n + 1)

                def last():
                    add(Lin(NB - 1), NT - 1)
                    invert(Lin(NB - 1))
                    sum_up(Lin(NB - 1))

                schedule(dve, first, one, last)

            @block.tensor
            def _(pe):
                freed = [None]

                def take_spare(sem_, value):
                    if freed[0]:
                        wait(pe, *freed[0])
                    freed[0] = (sem_, value)

                def turn_x(j):
                    pe.wait_ge(a_xn, j + 1)
                    for k in range(TB):
                        mm = pe.transpose(TX[j][:, k * P:(k + 1) * P], xn[:, j * TB + k, :], ident[:, :])
                    mm.then_inc(t_x, 1)

                def logits():
                    take_spare(v_mask, 1)
                    pe.wait_ge(d_c, 32)
                    for k in range(NT):
                        mm = pe.matmul(XB[:, k * E:(k + 1) * E], xT[:, k * P:(k + 1) * P], rw[:, :], start=True, stop=True)
                    mm.then_inc(t_lg, 1)

                def ranks():
                    take_spare(v_mask, 2)
                    pe.wait_ge(g_i, 6)
                    pe.wait_ge(v_mask, 1)
                    chosen = mask[:, :, :].rearrange("p e t -> p (e t)")
                    pe.matmul(XB[:, 0:NT * E], before_p[:, :], chosen, start=True, stop=True)
                    pe.matmul(XB[:, NT * E:2 * NT * E], ones[:, :], chosen, start=True, stop=True).then_inc(t_rk, 1)

                def turn_tokens(r):
                    take_spare(a_tok, r.times(1, 1))
                    wait(pe, d_tile, r.times(48, 48))
                    pe.transpose(XB[:, 0:P], tok[:, :], ident[:, :]).then_inc(t_tok, 1)

                def expert_up(r):
                    take_spare(a_up, r.times(1, 1))
                    wait(pe, a_tok, r.times(1, 1))
                    for c in range(NC):
                        mm = pe.matmul(XB[:, c * P:(c + 1) * P], w1[:, c * P:(c + 1) * P], tokT[:, :], start=True, stop=True)
                    mm.then_inc(t_up, 1)

                def expert_down(r):
                    take_spare(a_res, r.times(1, 1))
                    wait(pe, g_hid, r.times(1, 1))
                    for c in range(NC):
                        mm = pe.matmul(XB[:, 0:D], hid[:, c * P:(c + 1) * P], w2[:, c, :], start=(c == 0), stop=(c == NC - 1))
                    mm.then_inc(t_down, 1)

                def scores(n, kt):
                    par, k, keys = (n // JB) % 2, n % JB, slice(kt * P, (kt + 1) * P)
                    for h in range(2):
                        wait(pe, a_e, n.times(2 * NT, 2 * kt + h - 1))
                        if kt == 0:
                            q_ready(pe, n)
                        pe.matmul(SB[h][:, :], K1[par][h][:, keys], Q1[k][h][:, :], start=True, stop=False)
                        if kt == 0 and h == 0:
                            wait(pe, d_nm[k], (n // JB).times(32, 32))
                            wait(pe, g_c, 2)
                        pe.matmul(SB[h][:, :], K2[par][h][:, keys], Q2[k][h][:, :], start=False, stop=True).then_inc(t_s, 1)

                def max_unit(m, i, u=None):
                    u = i if u is None else u
                    h, q, half = u // 8, u % 8 // 2, u % 2
                    par, k = (m // JB) % 2, m % JB
                    wait(pe, v_m, m.times(UNITS, i - 1))
                    if i == 0:
                        q_ready(pe, m)
                        if m.i is not None or m.off:
                            k_ready(pe, m // JB)
                    for c in range(2):
                        keys = slice((2 * half + c) * QB, (2 * half + c + 1) * QB)
                        mm = pe.matmul(MB[i % 2][:, c * QB:(c + 1) * QB], Q1[k][h][:, q * P:(q + 1) * P],
                                       K1[par][h][:, keys], start=True, stop=True)
                    mm.then_inc(t_m, 1)

                def times_v(n, kt):
                    wait(pe, a_e, n.times(2 * NT, 2 * kt + 2))
                    if kt == 0:
                        wait(pe, a_o, n.times(1))
                        wait(pe, a_v, (n // JB).times(JB, JB))
                    for h in range(2):
                        mm = pe.matmul(OB[own[h], :], V[(n // JB) % 2][:, kt, own[h]], EX[h][kt % RING][:, :],
                                       start=(kt == 0), stop=(kt == NT - 1))
                    mm.then_inc(t_pv, 1)

                def split_product(w, par, c, XB):
                    q = slice(c * QB, (c + 1) * QB)
                    pe.matmul(XB[:, :], whi[par][:, w, :], xhi[:, q], start=True, stop=False)
                    pe.matmul(XB[:, :], wlo[par][:, w, :], xhi[:, q], start=False, stop=False)
                    return pe.matmul(XB[:, :], whi[par][:, w, :], xlo[:, q], start=False, stop=True)

                def make_q(m, bank=XB):
                    if bank is XB:
                        take_spare(v_q, m.times(1, 1))
                    wait(pe, v_w, (m // JB).times(1, 1))
                    split_product(0, (m // JB) % 2, m % JB, bank).then_inc(t_q, 1)

                def make_kv(kind, pair, c, bank=XB):
                    if kind == "k":
                        if bank is XB:
                            take_spare(v_k, pair.times(JB, c + 1))
                        wait(pe, v_w, pair.times(1, 1))
                        split_product(1, pair % 2, c, bank).then_inc(t_k, 1)
                    else:
                        take_spare(a_v, pair.times(JB, c + 1))
                        wait(pe, d_w[pair % 2], (pair // 2).times(48, 48))
                        for k in range(TB):
                            tok = slice((c * TB + k) * P, (c * TB + k + 1) * P)
                            mm = pe.matmul(XB[:, k * P:(k + 1) * P], xT[:, tok], wraw[pair % 2][:, 2, :],
                                           start=True, stop=True)
                        mm.then_inc(t_v, 1)

                def denominators(n):
                    take_spare(v_rd, n.times(1, 1))
                    wait(pe, v_a, n.times(NT - 1, NT - 1))
                    wait(pe, g_a, n.times(NT - 1, NT - 1))
                    for h in range(2):
                        mm = pe.matmul(XB[own[h], :], ones[:, 0:DH], acc[h][n % 2][:, :], start=True, stop=True)
                    mm.then_inc(t_den, 1)

                def project(n):
                    take_spare(v_y, n.times(1, 1))
                    pair = n // JB
                    wait(pe, g_on, n.times(1, 1))
                    wait(pe, d_wo[pair % 2], (pair // 2).times(16, 16))
                    for q in range(TB):
                        mm = pe.matmul(XB[:, q * P:(q + 1) * P], on[:, q * P:(q + 1) * P], wo_s[pair % 2][:, :],
                                       start=True, stop=True)
                    mm.then_inc(t_wo, 1)

                def turn_max(m):
                    take_spare(a_nm, m.times(1, 1))
                    wait(pe, v_nm, m.times(1, 1))
                    pe.transpose(XB[0:UNITS // 2, 0:P], nm[:, m % 2, :], ident[:, :]).then_inc(t_nm, 1)

                def first():
                    pe.wait_ge(g_i, 4)
                    for j in range(JB + 1):
                        if j < JB:
                            turn_x(j)
                        if j:
                            pe.wait_ge(v_lo, j)
                            make_kv("k", Lin(0), j - 1, START[j - 1])
                        if j == 2:
                            pe.wait_ge(v_k, 1)
                            make_q(Lin(0), SB[0])
                    pe.wait_ge(a_x, JB)
                    for u in range(UNITS):
                        if u in (0, UNITS // 2):
                            for c in (0, 1) if u == 0 else (2, 3):
                                pe.wait_ge(d_k0[c], 32)
                        max_unit(Lin(0), u, ORDER[u])
                        if u in BETWEEN:
                            kind, c = BETWEEN[u]
                            if kind == "v":
                                make_kv("v", Lin(0), c)
                            else:
                                make_q(Lin(c))
                    turn_max(Lin(0))
                    for u in range(LEAD):
                        max_unit(Lin(1), u)

                def one(n):
                    start = n.i is None and n.off == 0
                    if n.i is not None and n.off == 1:
                        freed[0] = (a_nm, n.times(1, 1))
                    for kt in range(NT):
                        scores(n, kt)
                        for m, u in (unit(n, kt - 1), unit(n, kt)) if kt % 2 else ():
                            if before(m, NB):
                                max_unit(m, u)
                        if kt == AT_DEN and not start:
                            denominators(n - 1)
                        if start and kt == AT_LOGIT:
                            logits()
                        if start and kt == AT_RANK:
                            ranks()
                        if has_tile(n):
                            if kt == AT_TOK:
                                turn_tokens(n - 1)
                            if kt == AT_UP:
                                expert_up(n - 1)
                            if kt == AT_DOWN:
                                expert_down(n - 1)
                        if kt in AT_KV and before(n, NB - JB):
                            make_kv(*kv_jobs(n)[AT_KV.index(kt)])
                        if kt == AT_Q and before(n, NB - 3):
                            make_q(n + 3)
                        if kt == AT_WO and not start:
                            project(n - 1)
                        if kt == AT_T and before(n, NB - 1):
                            turn_max(n + 1)
                        if n.i is None and n.off == NB - 1 and kt:
                            times_v(n, kt - 1)
                        elif kt % 2 == 0:
                            for d in (2, 1):
                                if kt:
                                    times_v(n, kt - d)
                                elif not start:
                                    times_v(n - 1, NT - d)
                    if n.i is not None and n.off == LOOP:
                        freed[0] = (a_nm, LOOP * TURNS + 2)

                def last():
                    times_v(Lin(NB - 1), NT - 1)
                    denominators(Lin(NB - 1))
                    project(Lin(NB - 1))

                schedule(pe, first, one, last)


def kernel(L0_attn_x, L0_attn_Wq, L0_attn_Wk, L0_attn_Wv, L0_attn_Wo, L0_attn_bo, L0_ffn_router_w, L0_ffn_expert_fc,
           L0_ffn_expert_proj):
    import concourse.bacc as bacc
    from concourse.bass_utils import run_bass_kernel_spmd

    nc = bacc.Bacc("TRN2", target_bir_lowering=False, num_devices=1)
    ins = {
        "x": L0_attn_x, "wq": L0_attn_Wq, "wk": L0_attn_Wk, "wv": L0_attn_Wv, "wo": L0_attn_Wo, "bo": L0_attn_bo,
        "router_wT": np.asarray(L0_ffn_router_w).T, "fc": L0_ffn_expert_fc,
        "projT": np.asarray(L0_ffn_expert_proj).transpose(0, 2, 1),
    }
    ins = {n: np.ascontiguousarray(a) for n, a in ins.items()}
    aps = [nc.dram_tensor(n, a.shape, mybir.dt.from_np(a.dtype), kind="ExternalInput").ap() for n, a in ins.items()]
    out = nc.dram_tensor("out", (1, S, D), F32, kind="ExternalOutput").ap()
    layer(nc, *aps, out)
    r = run_bass_kernel_spmd(nc, [ins], core_ids=[0])
    return r.results[0]["out"]
```

```python
from contextlib import ExitStack

import numpy as np

import concourse.bass as bass
from concourse import mybir

F32 = mybir.dt.float32
F32R = mybir.dt.float32r
U32 = mybir.dt.uint32
I32 = mybir.dt.int32
ALU = mybir.AluOpType
ACT = mybir.ActivationFunctionType
AX = mybir.AxisListType

S, D, H, DH = 2048, 128, 16, 64
E, HD = 8, 512
P = 128
NT = S // P
QB = 512
JB = S // QB
TB = QB // P
PAIRS = H // 2
NB = PAIRS * JB
NC = HD // P
SCALE = DH ** -0.5
EPS = 1e-5


class Lin:

    def __init__(self, off, coef=0, i=None):
        self.off, self.coef, self.i = off, (coef if i is not None else 0), i

    def __add__(self, k):
        return Lin(self.off + k, self.coef, self.i)

    def __sub__(self, k):
        return self + (-k)

    def __floordiv__(self, k):
        assert self.coef % k == 0
        return Lin(self.off // k, self.coef // k, self.i)

    def __mod__(self, k):
        assert self.coef % k == 0
        return self.off % k

    def place(self, a, r=0):
        v = a * self.off + r
        return v if self.i is None else self.i * (a * self.coef) + v

    def times(self, a, r=0):
        assert self.i is None or a * self.off + r >= 1
        return self.place(a, r)


def wait(eng, sem, value):
    if isinstance(value, int) and value <= 0:
        return
    eng.wait_ge(sem, value)


def address(eng, value):
    return value if isinstance(value, int) else eng.snap(value)


LEAD = 4
UNITS = 16
RING = 4
AT_DEN, AT_KV, AT_Q, AT_WO, AT_NM, AT_T = 2, (4, 10), 6, 8, 12, 13
AT_TOK, AT_UP, AT_DOWN = 5, 7, 11
LOOP = 8
TURNS = (NB - 1) // LOOP
TILES = LOOP * TURNS
assert TILES >= NT + E - 1
AT_Q2, AT_RANK = 3, 6
BACK = (4, 5, 6, 7)


def layer(nc, x, wq, wk, wv, wo, bo, router_wT, fc, projT, out):
    with ExitStack() as ctx:
        def sb(name, shape, dt=F32):
            return ctx.enter_context(nc.sbuf_tensor(name, shape, dt))

        def sem(name):
            return ctx.enter_context(nc.semaphore(name))

        def bank(name, n=1):
            return ctx.enter_context(nc.psum_tensor(name, [P, n * QB], F32))

        Y = sb("Y", [P, NT, D])
        xT, xhi, xlo = sb("xT", [P, S]), sb("xhi", [P, S], F32R), sb("xlo", [P, S], F32R)
        ident, ones = sb("ident", [P, P]), sb("ones", [P, P])

        own = [slice(0, DH), slice(DH, P)]
        other = [slice(DH, P), slice(0, DH)]
        maxrow = [slice(DH, DH + 1), slice(0, 1)]
        K1, K2 = ([[sb(f"{n}_{k}{h}", [P, S], F32R) for h in range(2)] for k in range(2)] for n in ("K1", "K2"))
        Q1, Q2 = ([[sb(f"{n}_{k}{h}", [P, QB], F32R) for h in range(2)] for k in range(JB)] for n in ("Q1", "Q2"))
        V = [sb(f"V{k}", [P, NT, P]) for k in range(2)]
        qhi, qlo, khi, klo = (sb(n, [P, QB], F32R) for n in ("qhi", "qlo", "khi", "klo"))
        wraw = [sb(f"wraw{k}", [P, 3, P]) for k in range(2)]
        whi = [sb(f"whi{k}", [P, 2, P], F32R) for k in range(2)]
        wlo = [sb(f"wlo{k}", [P, 2, P], F32R) for k in range(2)]
        wo_s = [sb(f"wo{k}", [P, D]) for k in range(2)]
        EX = [[sb(f"ex{h}{k}", [P, QB]) for k in range(RING)] for h in range(2)]
        acc = [[sb(f"acc{h}{k}", [P, QB]) for k in range(2)] for h in range(2)]
        xn = V[1]
        halves, mean_var = sb("halves", [P, NT, 6]), sb("mean_var", [P, NT, 2])
        std, rstd = sb("std", [P, NT]), sb("rstd", [P, NT])
        bob, eps = sb("bob", [P, D]), sb("eps", [P, 1])
        rw = sb("rw", [P, E])
        pick, mask, total, cum, place = (sb(n_, [P, E, NT]) for n_ in ("pick", "mask", "total", "cum", "place"))
        top, slot = sb("top", [P, NT]), sb("slot", [P, NT], U32)
        tiles_of, end, first_tile = (sb(n_, [P, E]) for n_ in ("tiles_of", "end", "first_tile"))
        past, owner, owner_i = sb("past", [P, TILES, E]), sb("owner", [P, TILES]), sb("owner_i", [P, TILES], I32)
        before_p, gate = sb("before_p", [P, P]), sb("gate", [P, E, NT])
        falling, tokens_in, tile_no, one_e = (
            sb(n_, [P, k]) for n_, k in (("falling", E), ("tokens_in", NT), ("tile_no", TILES), ("one_e", E)))
        tok, tokT, w1, w2 = sb("tok", [P, D]), sb("tokT", [P, P]), sb("w1", [P, HD]), sb("w2", [P, NC, D])
        up, hid, res = sb("up", [P, NC * P]), sb("hid", [P, NC * P]), sb("res", [P, D])
        sorted_x = nc.dram_tensor("sorted_x", (TILES * P, D), F32, kind="Internal").ap()
        sorted_y = nc.dram_tensor("sorted_y", (TILES * P, D), F32, kind="Internal").ap()
        osb, rd, on = sb("osb", [P, QB]), sb("rd", [P, QB]), sb("on", [P, QB])
        mx, nm = sb("mx", [P, 2, UNITS]), sb("nm", [P, 2, UNITS // 2])
        mrow = sb("mrow", [UNITS // 2, P], F32R)
        MB = [bank(f"MB{k}", 2) for k in range(2)]
        SB = [bank(f"SB{h}") for h in range(2)]
        OB, XB = bank("OB"), bank("XB")

        t_s, t_m, t_pv, t_q, t_k, t_v, t_den, t_wo, t_nm = (
            sem(f"t_{n}") for n in ("s", "m", "pv", "q", "k", "v", "den", "wo", "nm"))
        a_e, a_o, a_q, a_k, a_w, a_v, a_nm = (sem(f"a_{n}") for n in ("e", "o", "q", "k", "w", "v", "nm"))
        v_m, v_nm, v_q, v_k, v_w, v_a, v_rd, v_y = (
            sem(f"v_{n}") for n in ("m", "nm", "q", "k", "w", "a", "rd", "y"))
        g_a, g_on, g_c = sem("g_a"), sem("g_on"), sem("g_c")
        d_x, d_c = [sem(f"d_x{j}") for j in range(JB)], sem("d_c")
        v_half, v_mv, a_std, v_rs, v_xn, t_x, a_x, g_lo, g_y, g_i, g_z = (sem(n_) for n_ in (
            "v_half", "v_mv", "a_std", "v_rs", "v_xn", "t_x", "a_x", "g_lo", "g_y", "g_i", "g_z"))
        a_q0 = sem("a_q0")
        t_lg, t_rk, v_r, v_mask, v_slot, v_own, d_sort = (
            sem(n_) for n_ in ("t_lg", "t_rk", "v_r", "v_mask", "v_slot", "v_own", "d_sort"))
        d_tile, t_tok, t_up, t_down, a_tok, a_up, a_res, g_hid, d_res, d_back, v_back = (
            sem(n_) for n_ in ("d_tile", "t_tok", "t_up", "t_down", "a_tok", "a_up", "a_res", "g_hid", "d_res",
                               "d_back", "v_back"))
        d_q, d_nm = ([sem(f"d_{n}{k}") for k in range(JB)] for n in ("q", "nm"))
        d_k, d_w, d_wo = ([sem(f"d_{n}{k}") for k in range(2)] for n in ("k", "w", "wo"))
        d_k0 = [sem(f"d_k0{c}") for c in range(JB)]
        d_q0 = sem("d_q0_")
        v_on = sem("v_on")
        d_out = sem("d_out")
        QD, KD = 6 * 16, 6 * 16

        def unit(n, kt):
            g = UNITS + kt + LEAD
            return n + g // UNITS, g % UNITS

        def added(n, kt):
            return n.times(NT - 1, max(kt, 1))

        def kv_jobs(n):
            j = n % JB
            return [("k" if j < 2 else "v", n // JB + 1, 2 * (j % 2) + c) for c in range(2)]

        def q_jobs(n, kt):
            if n.i is None and n.off == 0:
                return [Lin(2)] * (kt == AT_Q2) + [Lin(3)] * (kt == AT_WO)
            return [n + 3] * (kt == AT_Q and before(n, NB - 3))

        def schedule(eng, first, block, last):
            first()
            block(Lin(0))
            with eng.Fori(0, TURNS) as i:
                for b in range(1, LOOP + 1):
                    block(Lin(b, LOOP, i))
            for n in range(1 + LOOP * TURNS, NB):
                block(Lin(n))
            last()

        def before(n, limit):
            return n.i is not None or n.off < limit

        def q_ready(eng, m):
            wait(eng, d_q[m % JB], (m // JB).times(QD, QD))

        BETWEEN = {1: ("v", 0), 3: ("v", 1), 5: ("v", 2), 7: ("v", 3), 9: ("q", 1),
                   10: ("r", 0), 11: ("r", 1), 12: ("r", 2), 13: ("r", 3)}
        START = [SB[0], SB[1], OB, XB]
        TX = [MB[j % 2][:, j // 2 * QB:(j // 2 + 1) * QB] for j in range(JB)]
        ORDER = list(range(0, UNITS, 2)) + list(range(1, UNITS, 2))

        LAST = [SB[0], SB[1], MB[0][:, 0:QB], MB[1][:, 0:QB]]

        def k_ready(eng, pair):
            wait(eng, d_k[pair % 2], (pair // 2).times(JB * KD, JB * KD))

        def chunk(a, j):
            return a[:, j * TB:(j + 1) * TB, :]

        def over(a, n):
            return a.unsqueeze(2).to_broadcast([P, a.shape[1], n])

        def under(a, n):
            return a.unsqueeze(1).to_broadcast([P, n, a.shape[1]])

        def has_tile(n):
            return n.i is not None or 0 < n.off <= TILES

        with nc.Block() as block:
            @block.sync
            def _(sp):
                def load_w(pair):
                    k, cols = pair % 2, bass.ds(address(sp, pair.place(P)), P)
                    wait(sp, t_v, pair.times(JB, -JB))
                    for n, w in enumerate((wq, wk, wv)):
                        sp.dma_start(wraw[k][:, n, :], w[:, cols]).then_inc(d_w[k], 16)

                def load_wo(pair):
                    rows = bass.ds(address(sp, pair.place(P)), P)
                    if pair.i is not None or pair.off:
                        wait(sp, t_wo, pair.times(JB, 1 - JB))
                    sp.dma_start(wo_s[pair % 2][:, :], wo[rows, :]).then_inc(d_wo[pair % 2], 16)

                def copy(dst, src, s):
                    sp.dma_start(dst.bitcast(F32), src.bitcast(F32)).then_inc(s, 16)

                def spread_q(m):
                    k = m % JB
                    wait(sp, v_q, m.times(1, 1))
                    for h in range(2):
                        copy(Q1[k][h][own[h], :], qhi[own[h], :], d_q[k])
                        copy(Q2[k][h][own[h], :], qhi[own[h], :], d_q[k])
                        copy(Q1[k][h][other[h], :], qlo[own[h], :], d_q[k])

                def spread_k(pair, c):
                    k, q = pair % 2, slice(c * QB, (c + 1) * QB)
                    wait(sp, v_k, pair.times(JB, c + 1))
                    for h in range(2):
                        copy(K1[k][h][own[h], q], khi[own[h], :], d_k[k])
                        copy(K1[k][h][other[h], q], khi[own[h], :], d_k[k])
                        copy(K2[k][h][own[h], q], klo[own[h], :], d_k[k])

                def spread_k0(c):
                    q = slice(c * QB, (c + 1) * QB)
                    sp.wait_ge(a_k, c + 1)
                    for h in range(2):
                        copy(K1[0][h][other[h], q], K1[0][h][own[h], q], d_k0[c])

                def spread_q0():
                    sp.wait_ge(v_q, 1)
                    for h in range(2):
                        copy(Q1[0][h][other[h], :], qlo[own[h], :], d_q0)

                def place_max(m):
                    k = m % JB
                    wait(sp, a_nm, m.times(1, 1))
                    wait(sp, g_c, 1)
                    for h in range(2):
                        copy(Q2[k][h][maxrow[h], :], mrow[h * TB:(h + 1) * TB, :], d_nm[k])

                def load_tile(r):
                    e = sp.value_load(owner_i[0:1, bass.ds(r.place(1), 1)], min_val=0, max_val=E - 1)
                    sp.dma_start(tok[:, :], sorted_x[bass.ds(r.place(P), P), :]).then_inc(d_tile, 16)
                    sp.dma_start(w1[:, :], fc[bass.ds(e, 1), :, :].rearrange("e d h -> d (e h)")).then_inc(d_tile, 16)
                    sp.dma_start(w2[:, :, :], projT[bass.ds(e, 1), :, :].rearrange("e (c p) d -> p (e c) d", p=P))\
                      .then_inc(d_tile, 16)

                def store_tile(r):
                    wait(sp, a_res, r.times(1, 1))
                    sp.dma_start(sorted_y[bass.ds(r.place(P), P), :], res[:, :]).then_inc(d_res, 16)

                def first():
                    xv = x.rearrange("o (t p) d -> p (o t) d", p=P)
                    for j in range(JB):
                        sp.dma_start(chunk(Y, j), chunk(xv, j)).then_inc(d_x[j], 16)
                    load_w(Lin(0))
                    sp.dma_start(rw[:, :], router_wT).then_inc(d_c, 16)
                    sp.dma_start(bob[:, :], bo.rearrange("(o d) -> o d", o=1).to_broadcast([P, D])).then_inc(d_c, 16)
                    for c in range(JB):
                        spread_k0(c)
                        if c == 0:
                            spread_q0()
                    load_w(Lin(1))
                    load_wo(Lin(0))
                    sp.wait_ge(d_q0, 32)
                    sp.wait_ge(a_q0, 1)
                    sp.sem_inc(d_q[0], QD)
                    for c in range(JB):
                        sp.wait_ge(d_k0[c], 32)
                    sp.wait_ge(v_k, JB)
                    sp.sem_inc(d_k[0], JB * KD)
                    spread_q(Lin(1))
                    sp.wait_ge(g_i, 1)
                    sp.dma_start(sorted_x.rearrange("(r p) d -> p r d", p=P), under(res[:, :], TILES)).then_inc(d_res, 16)
                    place_max(Lin(0))

                def one(n):
                    pair = n // JB
                    if has_tile(n):
                        sp.wait_ge(d_sort, 16 * NT)
                        sp.wait_ge(v_own, 1)
                        load_tile(n - 1)
                    if n % JB == 1:
                        if before(n, NB - 2 * JB):
                            load_w(pair + 2)
                        if before(n, NB - JB):
                            load_wo(pair + 1)
                    spread = kv_jobs(n) if before(n, NB - JB) and n % JB < 2 else [None, None]
                    if spread[0]:
                        spread_k(*spread[0][1:])
                    for kt in range(NT):
                        for m in q_jobs(n, kt):
                            spread_q(m)
                    if spread[1]:
                        spread_k(*spread[1][1:])
                    if has_tile(n):
                        store_tile(n - 1)
                    if before(n, NB - 1):
                        place_max(n + 1)

                def last():
                    ov = out.rearrange("o (t p) d -> p (o t) d", p=P)
                    for j in range(JB - 1):
                        sp.wait_ge(v_y, NB - JB + j + 1)
                        sp.dma_start(chunk(ov, j), chunk(Y, j)).then_inc(d_out, 16)
                    for q in range(TB):
                        k = NT - TB + q
                        sp.wait_ge(v_y, NB + q)
                        sp.dma_start(ov[:, k:k + 1, :], Y[:, k:k + 1, :]).then_inc(d_out, 16)
                    sp.wait_ge(d_out, 16 * (JB - 1 + TB))

                schedule(sp, first, one, last)

            @block.gpsimd
            def _(pool):
                def add(n, kt):
                    a = acc[1][n % 2]
                    wait(pool, a_e, n.times(2 * NT, 2 * kt + 2))
                    if kt == 1:
                        src = EX[1][0]
                    else:
                        wait(pool, g_a, n.times(NT - 1, kt - 1))
                        src = a
                    pool.tensor_tensor(a[:, :], src[:, :], EX[1][kt % RING][:, :], ALU.add).then_inc(g_a, 1)

                def normalise(n):
                    wait(pool, v_rd, n.times(1, 1))
                    wait(pool, a_o, n.times(1, 1))
                    pool.tensor_tensor(on[:, :], osb[:, :], rd[:, :], ALU.mult).then_inc(g_on, 1)

                def square(r):
                    wait(pool, a_up, r.times(1, 1))
                    pool.tensor_tensor(hid[:, :], up[:, :], up[:, :], ALU.mult).then_inc(g_hid, 1)

                def indexed(k):
                    return bass.IndirectOffsetOnAxis(ap=slot[:, k:k + 1], axis=0)

                def low_x(j):
                    q = slice(j * QB, (j + 1) * QB)
                    pool.wait_ge(a_x, j + 1)
                    pool.tensor_tensor(xlo[:, q], xT[:, q], xhi[:, q], ALU.subtract).then_inc(g_lo, 1)

                def sort_tokens(ks):
                    pool.wait_ge(v_slot, 1)
                    pool.wait_ge(d_res, 16)
                    for k in ks:
                        pool.indirect_dma_start(sorted_x, indexed(k), xn[:, k, :], None).then_inc(d_sort, 16)

                def fetch_results(ks):
                    pool.wait_ge(d_res, 16 * (TILES + 1))
                    pool.wait_ge(t_pv, NT * (NB - JB))
                    for k in ks:
                        pool.indirect_dma_start(V[0][:, k, :], None, sorted_y, indexed(k)).then_inc(d_back, 16)

                def first():
                    pool.memset(res[:, :], 0.0).then_inc(g_i, 1)
                    pool.memset(eps[:, :], EPS).then_inc(g_i, 1)
                    pool.memset(ident[:, :], 0.0).then_inc(g_i, 1)
                    pool.wait_ge(g_i, 3)
                    pool.affine_select(out=ident[:, :], in_=ident[:, :], compare_op=ALU.not_equal, fill=1.0,
                                       base=0, pattern=[[-1, P]], channel_multiplier=1).then_inc(g_i, 1)
                    pool.memset(ones[:, :], 1.0).then_inc(g_i, 1)
                    pool.wait_ge(g_i, 5)
                    pool.affine_select(out=before_p[:, :], in_=ones[:, :], compare_op=ALU.is_gt, fill=0.0,
                                       base=0, pattern=[[1, P]], channel_multiplier=-1)
                    pool.memset(one_e[:, :], 1.0)
                    pool.memset(gate[:, :, 1:NT], 1.0)
                    pool.memset(gate[:, :, 0:1], 0.0)
                    for a, n, step, base in ((falling, E, -1, E), (tokens_in, NT, P, 0), (tile_no, TILES, 1, 0)):
                        ins = pool.iota(a[:, :], [[step, n]], base=base, channel_multiplier=0,
                                        allow_small_or_imprecise_dtypes=True)
                    ins.then_inc(g_i, 1)
                    pool.wait_ge(g_i, 6)
                    zeros = [K2[0][h][other[h], :] for h in range(2)]
                    zeros += [Q2[k][h][other[h], :] for k in range(JB) for h in range(2)]
                    zeros += [K2[1][h][other[h], :] for h in range(2)]
                    for k, z in enumerate(zeros):
                        pool.memset(z.bitcast(F32), 0.0).then_inc(g_z, 1)
                        if k in (3, 5, 7, 9):
                            pool.wait_ge(g_z, k + 1)
                            low_x((k - 3) // 2)
                            pool.wait_ge(g_lo, (k - 1) // 2)
                    pool.wait_ge(g_z, len(zeros))
                    for h in range(2):
                        for k in range(2):
                            ins = pool.memset(K2[k][h][maxrow[h], :].bitcast(F32), 1.0)
                    ins.then_inc(g_c, 1)
                    pool.wait_ge(g_c, 1)
                    pool.wait_ge(d_c, 32)
                    for j in range(JB):
                        pool.wait_ge(v_xn, j + 1)
                        pool.tensor_tensor(chunk(Y, j), chunk(Y, j), under(bob[:, :], TB), ALU.add).then_inc(g_y, 1)

                def one(n):
                    for kt in range(1, NT):
                        add(n, kt)
                        if kt == 5 and not (n.i is None and n.off == 0):
                            normalise(n - 1)
                        if kt == AT_UP + 1 and has_tile(n):
                            square(n - 1)
                        if kt >= 8 and n.i is None and n.off == 0:
                            sort_tokens((2 * kt - NT, 2 * kt - NT + 1))
                        if n.i is None and n.off == NB - JB:
                            fetch_results((kt,) if kt > 1 else (0, 1))

                schedule(pool, first, one, lambda: None)

            @block.scalar
            def _(act):
                def exps(n, kt):
                    for h in range(2):
                        wait(act, t_s, n.times(2 * NT, 2 * kt + h + 1))
                        old = (n, kt - RING) if kt >= RING else (n - 1, kt - RING + NT)
                        if n.i is not None or n.off > 0 or kt >= RING:
                            wait(act, t_pv, old[0].times(NT, old[1] + 1))
                            wait(act, (v_a, g_a)[h], added(*old))
                        act.activation(EX[h][kt % RING][:, :], SB[h][:, :], ACT.Exp).then_inc(a_e, 1)

                def split_w(pair):
                    k = pair % 2
                    wait(act, d_w[k], (pair // 2).times(48, 48))
                    wait(act, t_q, pair.times(JB, -JB))
                    act.activation(whi[k][:, :, :], wraw[k][:, 0:2, :], ACT.Copy).then_inc(a_w, 1)

                def high_q(m):
                    wait(act, t_q, m.times(1, 1))
                    q_ready(act, m - 1)
                    act.activation(qhi[:, :], XB[:, :], ACT.Copy, scale=SCALE).then_inc(a_q, 1)

                def kv(kind, pair, c):
                    if kind == "k":
                        wait(act, t_k, pair.times(JB, c + 1))
                        if c:
                            wait(act, d_k[pair % 2], (pair // 2).times(JB * KD, c * KD))
                        else:
                            k_ready(act, pair - 1)
                        act.activation(khi[:, :], XB[:, :], ACT.Copy).then_inc(a_k, 1)
                    else:
                        wait(act, t_v, pair.times(JB, c + 1))
                        wait(act, t_pv, pair.times(NT * JB, 1 - NT * JB))
                        act.activation(V[pair % 2][:, c * TB:(c + 1) * TB, :].rearrange("p t d -> p (t d)"), XB[:, :],
                                       ACT.Copy).then_inc(a_v, 1)

                def max_rows(m):
                    wait(act, t_nm, m.times(1, 1))
                    if not (m.i is None and m.off == 0):
                        old = m - 1
                        wait(act, d_nm[old % JB], (old // JB).times(32, 32))
                    act.activation(mrow[:, :], XB[0:UNITS // 2, 0:P], ACT.Copy).then_inc(a_nm, 1)

                def take_o(n):
                    wait(act, t_pv, n.times(NT, NT))
                    act.activation(osb[:, :], OB[:, :], ACT.Copy).then_inc(a_o, 1)

                def root(j):
                    c = slice(j * TB, (j + 1) * TB)
                    act.wait_ge(v_mv, j + 1)
                    act.activation(std[:, c], mean_var[:, c, 1:2].rearrange("p t o -> p (t o)"), ACT.Sqrt,
                                   bias=eps[:, 0:1]).then_inc(a_std, 1)

                def turned(j):
                    q = slice(j * QB, (j + 1) * QB)
                    act.wait_ge(t_x, j + 1)
                    act.activation(xhi[:, q], TX[j], ACT.Copy)
                    act.activation(xT[:, q], TX[j], ACT.Copy).then_inc(a_x, 1)

                def high_k0(c):
                    act.wait_ge(t_k, c + 1)
                    for h in range(2):
                        ins = act.activation(K1[0][h][own[h], c * QB:(c + 1) * QB], START[c][own[h], :], ACT.Copy)
                    ins.then_inc(a_k, 1)

                def high_q0():
                    act.wait_ge(t_q, 1)
                    for h in range(2):
                        ins = act.activation(Q1[0][h][own[h], :], SB[0][own[h], :], ACT.Copy, scale=SCALE)
                    ins.then_inc(a_q, 1)

                def copy_q0():
                    act.wait_ge(a_q, 1)
                    for h in range(2):
                        ins = act.activation(Q2[0][h][own[h], :], Q1[0][h][own[h], :], ACT.Copy)
                    ins.then_inc(a_q0, 1)

                def copy_tokens(r):
                    wait(act, t_tok, r.times(1, 1))
                    act.activation(tokT[:, :], XB[:, 0:P], ACT.Copy).then_inc(a_tok, 1)

                def rectify(r):
                    wait(act, t_up, r.times(1, 1))
                    act.activation(up[:, :], XB[:, :], ACT.Relu).then_inc(a_up, 1)

                def take_result(r):
                    wait(act, t_down, r.times(1, 1))
                    wait(act, d_res, r.times(16, 16))
                    act.activation(res[:, :], XB[:, 0:D], ACT.Copy).then_inc(a_res, 1)

                def first():
                    act.wait_ge(g_i, 2)
                    act.activation(up[:, 0:1], eps[:, 0:1], ACT.Sqrt)
                    for s_ in range(JB + 3):
                        if s_ < JB:
                            root(s_)
                        if s_ == 1:
                            split_w(Lin(0))
                        if 2 <= s_ < 4:
                            turned(s_ - 2)
                        if s_ == JB:
                            turned(3)
                        if s_ >= 3:
                            high_k0(s_ - 3)
                        if s_ == 3:
                            turned(2)
                            high_q0()
                    copy_q0()
                    for u in range(UNITS):
                        if u in BETWEEN:
                            kind, c = BETWEEN[u]
                            if kind == "v":
                                kv("v", Lin(0), c)
                            elif kind == "q":
                                high_q(Lin(c))
                    max_rows(Lin(0))

                def one(n):
                    for kt in range(NT):
                        exps(n, kt)
                        if has_tile(n):
                            if kt == AT_TOK:
                                copy_tokens(n - 1)
                            if kt == AT_UP:
                                rectify(n - 1)
                            if kt == AT_DOWN:
                                take_result(n - 1)
                        if kt == 0 and not (n.i is None and n.off == 0):
                            take_o(n - 1)
                        if kt == 1 and n % JB == 0 and before(n, NB - JB):
                            split_w(n // JB + 1)
                        if kt in AT_KV and before(n, NB - JB):
                            kv(*kv_jobs(n)[AT_KV.index(kt)])
                        for m in q_jobs(n, kt):
                            high_q(m)
                        if kt == AT_T and before(n, NB - 1):
                            max_rows(n + 1)

                schedule(act, first, one, lambda: take_o(Lin(NB - 1)))

            @block.vector
            def _(dve):
                def maxima(m, i, u=None):
                    u = i if u is None else u
                    wait(dve, t_m, m.times(UNITS, i + 1))
                    dve.tensor_reduce(mx[:, m % 2, u:u + 1], MB[i % 2][:, :], AX.X, ALU.max).then_inc(v_m, 1)

                def minus_max(m):
                    wait(dve, v_m, m.times(UNITS, UNITS))
                    wait(dve, t_nm, m.times(1, -1))
                    dve.tensor_reduce(nm[:, m % 2, :], mx[:, m % 2, :].rearrange("p (a b) -> p a b", b=2), AX.X,
                                      ALU.max, negate=True).then_inc(v_nm, 1)

                def add(n, kt):
                    a = acc[0][n % 2]
                    wait(dve, a_e, n.times(2 * NT, 2 * kt + 1))
                    if kt == 1:
                        src = EX[0][0]
                    else:
                        wait(dve, v_a, n.times(NT - 1, kt - 1))
                        src = a
                    dve.tensor_tensor(a[:, :], src[:, :], EX[0][kt % RING][:, :], ALU.add).then_inc(v_a, 1)

                def low_w(pair):
                    k = pair % 2
                    wait(dve, a_w, pair.times(1, 1))
                    dve.tensor_tensor(wlo[k][:, :, :], wraw[k][:, 0:2, :], whi[k][:, :, :], ALU.subtract).then_inc(v_w, 1)

                def statistics(j):
                    tiles = range(j * TB, (j + 1) * TB)
                    dve.wait_ge(d_x[j], 16)
                    for k in tiles:
                        ins = dve.bn_stats(halves[:, k, :], Y[:, k, :])
                    ins.then_inc(v_half, 1)
                    dve.wait_ge(v_half, j + 1)
                    for k in tiles:
                        ins = dve.bn_aggr(mean_var[:, k, :], halves[:, k, :])
                    ins.then_inc(v_mv, 1)

                def rows(j):
                    c = slice(j * TB, (j + 1) * TB)
                    dve.wait_ge(a_std, j + 1)
                    dve.reciprocal(rstd[:, c], std[:, c]).then_inc(v_rs, 1)
                    dve.wait_ge(v_rs, j + 1)
                    for k in range(j * TB, (j + 1) * TB):
                        ins = dve.tensor_scalar(xn[:, k, :], Y[:, k, :], mean_var[:, k, 0:1], rstd[:, k:k + 1],
                                                ALU.subtract, ALU.mult)
                    ins.then_inc(v_xn, 1)

                def low_k0(c):
                    q = slice(c * QB, (c + 1) * QB)
                    dve.wait_ge(a_k, c + 1)
                    for h in range(2):
                        ins = dve.tensor_tensor(K2[0][h][own[h], q], START[c][own[h], :], K1[0][h][own[h], q], ALU.subtract)
                    ins.then_inc(v_k, 1)

                def low_q0():
                    dve.wait_ge(a_q, 1)
                    for h in range(2):
                        ins = dve.scalar_tensor_tensor(out=qlo[own[h], :], in0=SB[0][own[h], :], scalar=SCALE,
                                                       in1=Q1[0][h][own[h], :], op0=ALU.mult, op1=ALU.subtract)
                    ins.then_inc(v_q, 1)

                routed = [0]

                def step(ins):
                    routed[0] += 1
                    ins.then_inc(v_r, 1)
                    dve.wait_ge(v_r, routed[0])

                def choose():
                    logit = XB[:, 0:NT * E].rearrange("p (t e) -> p e t", e=E)
                    by_tile = logit.rearrange("p e t -> p t e")
                    dve.wait_ge(t_lg, 1)
                    dve.wait_ge(g_i, 6)
                    step(dve.tensor_reduce(top[:, :], by_tile, AX.X, ALU.max))
                    step(dve.tensor_tensor(pick[:, :, :], logit, under(top[:, :], E), ALU.is_equal))
                    step(dve.tensor_tensor(pick[:, :, :], pick[:, :, :], over(falling[:, :], NT), ALU.mult))
                    step(dve.tensor_reduce(top[:, :], pick[:, :, :].rearrange("p e t -> p t e"), AX.X, ALU.max))
                    dve.tensor_tensor(mask[:, :, :], pick[:, :, :], under(top[:, :], E), ALU.is_equal).then_inc(v_mask, 1)

                def rank():
                    earlier = XB[:, 0:NT * E].rearrange("p (e t) -> p e t", e=E)
                    dve.wait_ge(t_rk, 1)
                    step(dve.tensor_copy(total[:, :, :].rearrange("p e t -> p (e t)"), XB[:, NT * E:2 * NT * E]))
                    dve.tensor_copy(place[:, :, :], earlier).then_inc(v_mask, 1)
                    step(dve.tensor_tensor_scan(cum[:, :, :].rearrange("p e t -> p (e t)"),
                                                gate[:, :, :].rearrange("p e t -> p (e t)"),
                                                total[:, :, :].rearrange("p e t -> p (e t)"), 0.0, ALU.mult, ALU.add))
                    dve.wait_ge(v_mask, 2)
                    step(dve.tensor_tensor(place[:, :, :], place[:, :, :], cum[:, :, :], ALU.add))
                    step(dve.tensor_tensor(place[:, :, :], place[:, :, :], total[:, :, :], ALU.subtract))
                    step(dve.tensor_tensor(total[:, :, :], cum[:, :, NT - 1:NT].to_broadcast([P, E, NT]),
                                           under(tokens_in[:, :], E), ALU.is_gt))
                    step(dve.tensor_reduce(tiles_of[:, :], total[:, :, :], AX.X, ALU.add))
                    step(dve.tensor_tensor_scan(end[:, :], one_e[:, :], tiles_of[:, :], 0.0, ALU.mult, ALU.add))
                    step(dve.tensor_tensor(first_tile[:, :], end[:, :], tiles_of[:, :], ALU.subtract))
                    step(dve.scalar_tensor_tensor(out=place[:, :, :], in0=over(first_tile[:, :], NT), scalar=float(P),
                                                  in1=place[:, :, :], op0=ALU.mult, op1=ALU.add))
                    step(dve.tensor_tensor(place[:, :, :], place[:, :, :], mask[:, :, :], ALU.mult))
                    step(dve.tensor_reduce(top[:, :], place[:, :, :].rearrange("p e t -> p t e"), AX.X, ALU.add))
                    dve.tensor_copy(slot[:, :], top[:, :]).then_inc(v_slot, 1)
                    step(dve.tensor_tensor(past[:, :, :], over(tile_no[:, :], E), under(end[:, :], TILES), ALU.is_ge))
                    step(dve.tensor_reduce(owner[:, :], past[:, :, :], AX.X, ALU.add))
                    dve.tensor_scalar(owner_i[:, :], owner[:, :], float(E - 1), None, ALU.min).then_inc(v_own, 1)

                def take_back(j):
                    dve.wait_ge(d_back, 16 * NT)
                    dve.wait_ge(v_y, NB - JB)
                    dve.tensor_tensor(chunk(Y, j), chunk(Y, j), chunk(V[0], j), ALU.add).then_inc(v_back, 1)

                def low_q(m):
                    wait(dve, a_q, m.times(1, 1))
                    dve.scalar_tensor_tensor(out=qlo[:, :], in0=XB[:, :], scalar=SCALE, in1=qhi[:, :],
                                             op0=ALU.mult, op1=ALU.subtract).then_inc(v_q, 1)

                def low_k(pair, c):
                    wait(dve, a_k, pair.times(JB, c + 1))
                    dve.tensor_tensor(klo[:, :], XB[:, :], khi[:, :], ALU.subtract).then_inc(v_k, 1)

                def invert(n):
                    wait(dve, t_den, n.times(1, 1))
                    dve.reciprocal(rd[:, :], XB[:, :]).then_inc(v_rd, 1)

                def sum_up(n):
                    wait(dve, t_wo, n.times(1, 1))
                    if n.i is None and n.off == NB - JB:
                        dve.wait_ge(v_back, JB)
                    y = Y[:, (n % JB) * TB:(n % JB + 1) * TB, :].rearrange("p t d -> p (t d)")
                    dve.tensor_tensor(y, XB[:, :], y, ALU.add).then_inc(v_y, 1)

                def first():
                    statistics(0)
                    statistics(1)
                    for s_ in range(1, JB + 3):
                        if s_ < JB:
                            rows(s_ - 1)
                        if s_ == JB - 1:
                            rows(s_)
                        if s_ < JB - 1:
                            statistics(s_ + 1)
                        if s_ == 1:
                            low_w(Lin(0))
                        if s_ >= 3:
                            low_k0(s_ - 3)
                        if s_ == 3:
                            low_q0()
                    for u in range(UNITS):
                        maxima(Lin(0), u, ORDER[u])
                        if u in BETWEEN:
                            kind, c = BETWEEN[u]
                            if kind == "q":
                                low_q(Lin(c))
                            elif kind == "r" and c == JB - 1:
                                choose()
                    minus_max(Lin(0))
                    for u in range(LEAD - 1):
                        maxima(Lin(1), u)

                def one(n):
                    start = n.i is None and n.off == 0
                    for kt in range(NT):
                        m, u = unit(n, kt - 1)
                        if before(m, NB):
                            maxima(m, u)
                        if kt > 1:
                            add(n, kt - 1)
                        if kt == 0 and not start:
                            add(n - 1, NT - 1)
                        if kt == 1 and n % JB == 0 and before(n, NB - JB):
                            low_w(n // JB + 1)
                        if kt == AT_DEN and not start:
                            invert(n - 1)
                        if kt in AT_KV and before(n, NB - JB):
                            kind, pair, c = kv_jobs(n)[AT_KV.index(kt)]
                            if kind == "k":
                                low_k(pair, c)
                        if start and kt == AT_RANK:
                            rank()
                        if n.i is None and n.off == NB - JB + 1 and kt in BACK:
                            take_back(BACK.index(kt))
                        for m in q_jobs(n, kt):
                            low_q(m)
                        if kt == AT_WO:
                            if start:
                                dve.wait_ge(g_y, JB)
                            else:
                                sum_up(n - 1)
                        if kt == AT_NM and before(n, NB - 1):
                            minus_max(n + 1)

                def last():
                    def cols(q):
                        return slice(q * P, (q + 1) * P)

                    def invert_tile(q):
                        dve.reciprocal(rd[:, cols(q)], XB[:, cols(q)]).then_inc(v_rd, 1)

                    def normalise_tile(q):
                        dve.wait_ge(v_rd, NB + q)
                        dve.wait_ge(a_o, NB)
                        dve.tensor_tensor(on[:, cols(q)], osb[:, cols(q)], rd[:, cols(q)], ALU.mult).then_inc(v_on, 1)

                    def sum_tile(q):
                        y = Y[:, NT - TB + q, :]
                        dve.wait_ge(t_wo, NB + q)
                        dve.tensor_tensor(y, LAST[q][:, 0:P], y, ALU.add).then_inc(v_y, 1)

                    add(Lin(NB - 1), NT - 1)
                    dve.wait_ge(t_den, NB)
                    for q in range(TB + 2):
                        if q < TB:
                            invert_tile(q)
                        if 1 <= q < TB + 1:
                            normalise_tile(q - 1)
                        if q >= 2:
                            sum_tile(q - 2)

                schedule(dve, first, one, last)

            @block.tensor
            def _(pe):
                freed = [None]

                def take_spare(sem_, value):
                    if freed[0]:
                        wait(pe, *freed[0])
                    freed[0] = (sem_, value)

                def turn_x(j):
                    pe.wait_ge(v_xn, j + 1)
                    for k in range(TB):
                        mm = pe.transpose(TX[j][:, k * P:(k + 1) * P], xn[:, j * TB + k, :], ident[:, :])
                    mm.then_inc(t_x, 1)

                def logits(j):
                    if j == 0:
                        take_spare(v_mask, 1)
                        pe.wait_ge(d_c, 32)
                    for k in range(j * TB, (j + 1) * TB):
                        mm = pe.matmul(XB[:, k * E:(k + 1) * E], xT[:, k * P:(k + 1) * P], rw[:, :], start=True, stop=True)
                    if j == JB - 1:
                        mm.then_inc(t_lg, 1)

                def ranks():
                    take_spare(v_mask, 2)
                    pe.wait_ge(g_i, 6)
                    pe.wait_ge(v_mask, 1)
                    chosen = mask[:, :, :].rearrange("p e t -> p (e t)")
                    pe.matmul(XB[:, 0:NT * E], before_p[:, :], chosen, start=True, stop=True)
                    pe.matmul(XB[:, NT * E:2 * NT * E], ones[:, :], chosen, start=True, stop=True).then_inc(t_rk, 1)

                def turn_tokens(r):
                    take_spare(a_tok, r.times(1, 1))
                    wait(pe, d_tile, r.times(48, 48))
                    pe.transpose(XB[:, 0:P], tok[:, :], ident[:, :]).then_inc(t_tok, 1)

                def expert_up(r):
                    take_spare(a_up, r.times(1, 1))
                    wait(pe, a_tok, r.times(1, 1))
                    for c in range(NC):
                        mm = pe.matmul(XB[:, c * P:(c + 1) * P], w1[:, c * P:(c + 1) * P], tokT[:, :], start=True, stop=True)
                    mm.then_inc(t_up, 1)

                def expert_down(r):
                    take_spare(a_res, r.times(1, 1))
                    wait(pe, g_hid, r.times(1, 1))
                    for c in range(NC):
                        mm = pe.matmul(XB[:, 0:D], hid[:, c * P:(c + 1) * P], w2[:, c, :], start=(c == 0), stop=(c == NC - 1))
                    mm.then_inc(t_down, 1)

                def scores(n, kt):
                    par, k, keys = (n // JB) % 2, n % JB, slice(kt * P, (kt + 1) * P)
                    for h in range(2):
                        wait(pe, a_e, n.times(2 * NT, 2 * kt + h - 1))
                        if kt == 0:
                            q_ready(pe, n)
                        pe.matmul(SB[h][:, :], K1[par][h][:, keys], Q1[k][h][:, :], start=True, stop=False)
                        if kt == 0 and h == 0:
                            wait(pe, d_nm[k], (n // JB).times(32, 32))
                            wait(pe, g_c, 1)
                        pe.matmul(SB[h][:, :], K2[par][h][:, keys], Q2[k][h][:, :], start=False, stop=True).then_inc(t_s, 1)

                def max_unit(m, i, u=None):
                    u = i if u is None else u
                    h, q, half = u // 8, u % 8 // 2, u % 2
                    par, k = (m // JB) % 2, m % JB
                    wait(pe, v_m, m.times(UNITS, i - 1))
                    if i == 0 and (m.i is not None or m.off):
                        q_ready(pe, m)
                        k_ready(pe, m // JB)
                    for c in range(2):
                        keys = slice((2 * half + c) * QB, (2 * half + c + 1) * QB)
                        mm = pe.matmul(MB[i % 2][:, c * QB:(c + 1) * QB], Q1[k][h][:, q * P:(q + 1) * P],
                                       K1[par][h][:, keys], start=True, stop=True)
                    mm.then_inc(t_m, 1)

                def times_v(n, kt, tiles):
                    wait(pe, a_e, n.times(2 * NT, 2 * (kt + tiles)))
                    if kt == 0:
                        wait(pe, a_o, n.times(1))
                        wait(pe, a_v, (n // JB).times(JB, JB))
                    for k in range(kt, kt + tiles):
                        for h in (0, 1) if k == kt else (1, 0):
                            mm = pe.matmul(OB[own[h], :], V[(n // JB) % 2][:, k, own[h]], EX[h][k % RING][:, :],
                                           start=(k == 0), stop=(k == NT - 1))
                    mm.then_inc(t_pv, tiles)

                def split_product(w, par, c, XB):
                    q = slice(c * QB, (c + 1) * QB)
                    pe.matmul(XB[:, :], whi[par][:, w, :], xhi[:, q], start=True, stop=False)
                    pe.matmul(XB[:, :], wlo[par][:, w, :], xhi[:, q], start=False, stop=False)
                    return pe.matmul(XB[:, :], whi[par][:, w, :], xlo[:, q], start=False, stop=True)

                def make_q(m, bank=XB):
                    if bank is XB:
                        take_spare(v_q, m.times(1, 1))
                    wait(pe, v_w, (m // JB).times(1, 1))
                    split_product(0, (m // JB) % 2, m % JB, bank).then_inc(t_q, 1)

                def make_kv(kind, pair, c, bank=XB):
                    if kind == "k":
                        if bank is XB:
                            take_spare(v_k, pair.times(JB, c + 1))
                        wait(pe, v_w, pair.times(1, 1))
                        split_product(1, pair % 2, c, bank).then_inc(t_k, 1)
                    else:
                        take_spare(a_v, pair.times(JB, c + 1))
                        wait(pe, d_w[pair % 2], (pair // 2).times(48, 48))
                        for k in range(TB):
                            tok = slice((c * TB + k) * P, (c * TB + k + 1) * P)
                            mm = pe.matmul(XB[:, k * P:(k + 1) * P], xT[:, tok], wraw[pair % 2][:, 2, :],
                                           start=True, stop=True)
                        mm.then_inc(t_v, 1)

                def denominators(n):
                    take_spare(v_rd, n.times(1, 1))
                    wait(pe, v_a, n.times(NT - 1, NT - 1))
                    wait(pe, g_a, n.times(NT - 1, NT - 1))
                    for h in range(2):
                        mm = pe.matmul(XB[own[h], :], ones[:, 0:DH], acc[h][n % 2][:, :], start=True, stop=True)
                    mm.then_inc(t_den, 1)

                def project(n):
                    take_spare(v_y, n.times(1, 1))
                    pair = n // JB
                    wait(pe, g_on, n.times(1, 1))
                    wait(pe, d_wo[pair % 2], (pair // 2).times(16, 16))
                    for q in range(TB):
                        mm = pe.matmul(XB[:, q * P:(q + 1) * P], on[:, q * P:(q + 1) * P], wo_s[pair % 2][:, :],
                                       start=True, stop=True)
                    mm.then_inc(t_wo, 1)

                def turn_max(m):
                    take_spare(a_nm, m.times(1, 1))
                    wait(pe, v_nm, m.times(1, 1))
                    pe.transpose(XB[0:UNITS // 2, 0:P], nm[:, m % 2, :], ident[:, :]).then_inc(t_nm, 1)

                def first():
                    pe.wait_ge(g_i, 4)
                    for j in range(JB + 1):
                        if j < JB:
                            turn_x(j)
                        if j == 3:
                            pe.wait_ge(v_k, 1)
                            make_q(Lin(0), SB[0])
                        if j:
                            pe.wait_ge(g_lo, j)
                            make_kv("k", Lin(0), j - 1, START[j - 1])
                    pe.wait_ge(a_x, JB)
                    pe.wait_ge(d_q0, 32)
                    for u in range(UNITS):
                        if u in (0, UNITS // 2):
                            for c in (0, 1) if u == 0 else (2, 3):
                                pe.wait_ge(d_k0[c], 32)
                        max_unit(Lin(0), u, ORDER[u])
                        if u in BETWEEN:
                            kind, c = BETWEEN[u]
                            if kind == "v":
                                make_kv("v", Lin(0), c)
                            elif kind == "q":
                                make_q(Lin(c))
                            else:
                                logits(c)
                    turn_max(Lin(0))
                    for u in range(LEAD):
                        max_unit(Lin(1), u)

                def one(n):
                    start = n.i is None and n.off == 0
                    if n.i is not None and n.off == 1:
                        freed[0] = (a_nm, n.times(1, 1))
                    for kt in range(NT):
                        scores(n, kt)
                        for m, u in (unit(n, kt - 1), unit(n, kt)) if kt % 2 else ():
                            if before(m, NB):
                                max_unit(m, u)
                        if kt == AT_DEN and not start:
                            denominators(n - 1)
                        if start and kt == AT_RANK:
                            ranks()
                        if has_tile(n):
                            if kt == AT_TOK:
                                turn_tokens(n - 1)
                            if kt == AT_UP:
                                expert_up(n - 1)
                            if kt == AT_DOWN:
                                expert_down(n - 1)
                        if kt in AT_KV and before(n, NB - JB):
                            make_kv(*kv_jobs(n)[AT_KV.index(kt)])
                        for m in q_jobs(n, kt):
                            make_q(m)
                        if kt == AT_WO and not start:
                            project(n - 1)
                        if kt == AT_T and before(n, NB - 1):
                            turn_max(n + 1)
                        if n.i is None and n.off == NB - 1 and kt:
                            times_v(n, kt - 1, 1)
                        elif kt % 2 == 0:
                            if kt:
                                times_v(n, kt - 2, 2)
                            elif not start:
                                times_v(n - 1, NT - 2, 2)
                    if n.i is not None and n.off == LOOP:
                        freed[0] = (a_nm, LOOP * TURNS + 2)

                def last():
                    times_v(Lin(NB - 1), NT - 1, 1)
                    denominators(Lin(NB - 1))
                    pe.wait_ge(v_m, UNITS * NB)
                    for q in range(TB):
                        pe.wait_ge(v_on, q + 1)
                        pe.matmul(LAST[q][:, 0:P], on[:, q * P:(q + 1) * P], wo_s[(PAIRS - 1) % 2][:, :],
                                  start=True, stop=True).then_inc(t_wo, 1)

                schedule(pe, first, one, last)


def kernel(L0_attn_x, L0_attn_Wq, L0_attn_Wk, L0_attn_Wv, L0_attn_Wo, L0_attn_bo, L0_ffn_router_w, L0_ffn_expert_fc,
           L0_ffn_expert_proj):
    import concourse.bacc as bacc
    from concourse.bass_utils import run_bass_kernel_spmd

    nc = bacc.Bacc("TRN2", target_bir_lowering=False, num_devices=1)
    ins = {
        "x": L0_attn_x, "wq": L0_attn_Wq, "wk": L0_attn_Wk, "wv": L0_attn_Wv, "wo": L0_attn_Wo, "bo": L0_attn_bo,
        "router_wT": np.asarray(L0_ffn_router_w).T, "fc": L0_ffn_expert_fc,
        "projT": np.asarray(L0_ffn_expert_proj).transpose(0, 2, 1),
    }
    ins = {n: np.ascontiguousarray(a) for n, a in ins.items()}
    aps = [nc.dram_tensor(n, a.shape, mybir.dt.from_np(a.dtype), kind="ExternalInput").ap() for n, a in ins.items()]
    out = nc.dram_tensor("out", (1, S, D), F32, kind="ExternalOutput").ap()
    layer(nc, *aps, out)
    r = run_bass_kernel_spmd(nc, [ins], core_ids=[0])
    return r.results[0]["out"]
```
